# Optimizing a Trainium2 kernel written in Bass

```python
import numpy as np
import jax
import jax.numpy as jnp

def _softmax(x, axis=-1):
    return jax.nn.softmax(x, axis=axis)

def _gelu(x):
    return jax.nn.gelu(x, approximate=True)

def _silu(x):
    return jax.nn.silu(x)

def _sigmoid(x):
    return jax.nn.sigmoid(x)

def _layernorm(x, axis=-1, eps=1e-05):
    m = jnp.mean(x, axis=axis, keepdims=True)
    v = jnp.var(x, axis=axis, keepdims=True)
    return (x - m) / jnp.sqrt(v + eps)

def _scatter_add(tgt, idx, src, axis=0):
    return tgt.at[idx].add(src)

def _segment_sum(src, seg, n):
    return jax.ops.segment_sum(src, seg, n)
kernel_name = 'mk_gnn_ffn_d1_gnn_r8_70e40d'

def setup_inputs(seed: int=0):
    np.random.seed(seed)
    _w = jnp.asarray

    def _rec_inputs():
        import jax
        import jax.numpy as jnp
        _gk = jax.random.key(seed)
        x = -0.0003713 + 1 * jax.random.normal(jax.random.fold_in(_gk, 1), (6250, 256), jnp.float32)
        _s = jax.random.randint(jax.random.fold_in(_gk, 2), (100000,), 0, 6250, jnp.int32)
        _d = jax.random.randint(jax.random.fold_in(_gk, 3), (100000,), 0, 6250, jnp.int32)
        _loop = jnp.arange(6250, dtype=jnp.int32)
        src = jnp.concatenate([_s, _d, _loop])
        dst = jnp.concatenate([_d, _s, _loop])
        _o = jnp.argsort(dst, stable=True)
        src = src[_o]
        dst = dst[_o]
        edge_type_8 = jax.random.randint(jax.random.fold_in(_gk, 12), (206250,), 0, 8, jnp.int32)
        return (x, src, dst, edge_type_8)
    x, src, dst, edge_type_8 = _rec_inputs()

    def _L0_gnn_setup():
        import jax, jax.numpy as jnp
        import numpy as np
        N_NODES = 6250
        N_EDGES = 100000
        IN_FEAT = 256
        OUT_FEAT = 256
        NUM_RELS = 8
        ALPHA = 0.5
        key = jax.random.key(seed)
        k1, k2, k3, k4, k5, k6 = jax.random.split(key, 6)
        x = jax.random.normal(k1, (N_NODES, IN_FEAT), dtype=jnp.float32)
        edge_index = jax.random.randint(k2, (2, N_EDGES), 0, N_NODES, dtype=jnp.int64)
        edge_type = jax.random.randint(k3, (N_EDGES,), 0, NUM_RELS, dtype=jnp.int64)
        gain = float(np.sqrt(2.0))
        lim_w = gain * float(np.sqrt(6.0 / (IN_FEAT + OUT_FEAT)))
        weight = jax.random.uniform(k4, (NUM_RELS, IN_FEAT, OUT_FEAT), dtype=jnp.float32, minval=-lim_w, maxval=lim_w)
        loop_weight = jax.random.uniform(k5, (IN_FEAT, OUT_FEAT), dtype=jnp.float32, minval=-lim_w, maxval=lim_w)
        h_bias = jnp.zeros((OUT_FEAT,), dtype=jnp.float32)
        return {'edge_index': edge_index, 'x': x, 'edge_type': edge_type, 'weight': weight, 'h_bias': h_bias, 'loop_weight': loop_weight}
    _L0_gnn_all = _L0_gnn_setup()
    _L0_gnn_in = {k: v for k, v in _L0_gnn_all.items() if k in ('weight', 'h_bias', 'loop_weight')}
    del _L0_gnn_all

    def _L0_ffn_setup():
        import jax, jax.numpy as jnp
        import numpy as np
        B, S, D = (8, 512, 256)
        H = 4 * D
        CAPACITY = 0.5
        key = jax.random.key(seed)
        ks = jax.random.split(key, 6)
        x = jax.random.normal(ks[0], (B, S, D), dtype=jnp.float32)
        attention_mask = jnp.zeros((B, 1, 1, S), dtype=jnp.float32)
        wr = jax.random.normal(ks[1], (D, 1), dtype=jnp.float32) * 0.02
        br = jnp.zeros((1,), dtype=jnp.float32)
        w1 = jax.random.normal(ks[2], (D, H), dtype=jnp.float32) * 0.02
        b1 = jnp.zeros((H,), dtype=jnp.float32)
        w2 = jax.random.normal(ks[3], (H, D), dtype=jnp.float32) * 0.02
        b2 = jnp.zeros((D,), dtype=jnp.float32)
        return {'x': x, 'attention_mask': attention_mask, 'wr': wr, 'br': br, 'w1': w1, 'b1': b1, 'w2': w2, 'b2': b2}
    _L0_ffn_all = _L0_ffn_setup()
    _L0_ffn_in = {k: v for k, v in _L0_ffn_all.items() if k in ('attention_mask', 'wr', 'br', 'w1', 'b1', 'w2', 'b2')}
    del _L0_ffn_all
    return {'x': x, 'src': src, 'dst': dst, 'edge_type_8': edge_type_8, 'L0_gnn_weight': _L0_gnn_in['weight'], 'L0_gnn_h_bias': _L0_gnn_in['h_bias'], 'L0_gnn_loop_weight': _L0_gnn_in['loop_weight'], 'L0_ffn_attention_mask': _L0_ffn_in['attention_mask'], 'L0_ffn_wr': _L0_ffn_in['wr'], 'L0_ffn_br': _L0_ffn_in['br'], 'L0_ffn_w1': _L0_ffn_in['w1'], 'L0_ffn_b1': _L0_ffn_in['b1'], 'L0_ffn_w2': _L0_ffn_in['w2'], 'L0_ffn_b2': _L0_ffn_in['b2']}

def reference(x, src, dst, edge_type_8, L0_gnn_weight, L0_gnn_h_bias, L0_gnn_loop_weight, L0_ffn_attention_mask, L0_ffn_wr, L0_ffn_br, L0_ffn_w1, L0_ffn_b1, L0_ffn_w2, L0_ffn_b2):
    import jax
    import jax.numpy as jnp

    def _L0_gnn_ref(edge_index, x, edge_type, weight, h_bias, loop_weight):
        import jax, jax.numpy as jnp
        import numpy as np
        N_NODES = 6250
        N_EDGES = 100000
        IN_FEAT = 256
        OUT_FEAT = 256
        NUM_RELS = 8
        ALPHA = 0.5
        num_nodes = x.shape[0]
        src, dst = (edge_index[0], edge_index[1])
        hx = jnp.einsum('ni,rio->rno', x, weight)
        msg = hx[edge_type, src]
        agg = jax.ops.segment_sum(msg, dst, num_segments=num_nodes)
        node_repr = agg * jnp.asarray(ALPHA, x.dtype) ** 0.5
        node_repr = node_repr + h_bias
        loop_message = x @ loop_weight
        node_repr = node_repr + loop_message * jnp.asarray(1.0 - ALPHA, x.dtype) ** 0.5
        return node_repr

    def _L0_ffn_ref(x, attention_mask, wr, br, w1, b1, w2, b2):
        import jax, jax.numpy as jnp
        import numpy as np
        B, S, D = (8, 512, 256)
        H = 4 * D
        CAPACITY = 0.5
        b, s, d = x.shape
        weights = (jnp.einsum('bsd,do->bso', x, wr) + br)[..., 0]
        k = max(1, int(CAPACITY * s))
        kk = k - 1 if k > 1 else 1
        _, idx = jax.lax.top_k(weights, k)
        sel_idx = idx[:, :kk]
        sel = jnp.take_along_axis(x, sel_idx[:, :, None], axis=1)
        h = jax.nn.gelu(jnp.einsum('bkd,dh->bkh', sel, w1) + b1)
        y = jnp.einsum('bkh,hd->bkd', h, w2) + b2
        w_sel = jnp.take_along_axis(weights, sel_idx, axis=1)
        y = y * w_sel[..., None]
        batch_idx = jnp.arange(b)[:, None]
        processed = jnp.zeros_like(x).at[batch_idx, sel_idx].set(y)
        return processed + x
    edge_index = jnp.stack([src, dst])
    x = x + _L0_gnn_ref(edge_index, _layernorm(x, axis=-1), edge_type_8, L0_gnn_weight, L0_gnn_h_bias, L0_gnn_loop_weight)
    x = x + _L0_ffn_ref(_layernorm(x, axis=-1)[None], L0_ffn_attention_mask, L0_ffn_wr, L0_ffn_br, L0_ffn_w1, L0_ffn_b1, L0_ffn_w2, L0_ffn_b2)[0]
    return x

_drawn_inputs = setup_inputs


def setup_inputs(seed=0):
    import zlib

    import numpy as np

    out = dict(_drawn_inputs(seed))
    spreads = {'L0_gnn_h_bias': (0.0, 0.467), 'L0_ffn_b1': (0.0, 0.8), 'L0_ffn_b2': (0.0, 0.8)}
    factors = {'L0_ffn_wr': 8.0, 'L0_ffn_w1': 8.0, 'L0_ffn_w2': 8.0}
    for name, (base, spread) in spreads.items():
        noise = np.random.default_rng([zlib.crc32(name.encode()), seed]).standard_normal(out[name].shape)
        drawn = base * np.exp(spread * noise) if base else spread * noise
        out[name] = jnp.asarray(drawn.astype(out[name].dtype))
    for name, factor in factors.items():
        out[name] = (out[name] * factor).astype(out[name].dtype)
    return out
```

```python
import concourse.bass as bass
from concourse import mybir
from contextlib import ExitStack

P = 128
F32 = mybir.dt.float32
I32 = mybir.dt.int32
ALU = mybir.AluOpType
ACT = mybir.ActivationFunctionType
AX = mybir.AxisListType


def gnn_ffn_program(nc, x, src, dst, edge_type, rel_w, h_bias, loop_w, wr, br, w1, b1, w2, b2, out):
    N, D = x.shape
    E = src.shape[0]
    R = rel_w.shape[0]
    H = w1.shape[1]
    KC = D // P
    HC = H // P
    NB = -(-N // P)
    LAST = N - (NB - 1) * P
    J = 4
    GE = J * P
    SLOTS = 4
    NG_FULL = E // GE
    NG = -(-(-(-E // GE)) // SLOTS) * SLOTS
    ROUNDS = NG // SLOTS
    GT = 4
    NGP = GT * P
    assert NG + SLOTS <= NGP and NB % 2 == 1
    SELECTED = max(1, int(0.5 * N)) - 1
    SCALE = 0.7071067811865476
    EPS = 1e-5
    TW = R * D
    BANK = 512

    ctx = ExitStack()
    with ctx:
        def sb(name, shape, dt=F32):
            return ctx.enter_context(nc.sbuf_tensor(name, shape, dt))

        def sem(name):
            return ctx.enter_context(nc.semaphore(name))

        table = nc.dram_tensor("message_table", [NB * P * R, D], F32).ap()
        table_blocks = table.rearrange("(b p r) d -> b p (r d)", p=P, r=R)

        acc = sb("acc", [P, NB + 1, D])
        nodes = sb("nodes", [P, NB, D])
        messages = sb("messages", [P, SLOTS, J * D])
        weights = sb("weights", [P, KC * (TW + D)])
        gather_rows = sb("gather_rows", [P, NGP, J], I32)
        window_keys = sb("window_keys", [P, NGP, J])
        wide_keys = sb("wide_keys", [P, NGP, J])
        natural = acc[:, 0:48, :].rearrange("p b d -> p (b d)")
        SL = GT * GE

        def slab(k, dt=F32):
            return natural[:, k * SL:(k + 1) * SL].bitcast(dt) if dt is not F32 else natural[:, k * SL:(k + 1) * SL]

        src_nat, type_nat, dst_nat = (slab(k, I32) for k in range(3))
        row_nat, dst_f, key_nat = (slab(k) for k in (3, 4, 5))
        masked_i, valid_f, bit_f = slab(0, I32), slab(1), slab(0)
        stage = messages[:, :, :].rearrange("p s d -> p (s d)").rearrange("p (u c) -> p u c", u=2)
        rel_sb = weights[:, :].rearrange("p (k c) -> p k c", k=KC)
        w1_sb = weights[:, 0:KC * H].rearrange("p (k h) -> p k h", k=KC)
        w2_sb = weights[:, KC * H:KC * H + HC * D].rearrange("p (m d) -> p m d", m=HC)

        onehot = sb("onehot", [P, SLOTS, J, P])
        hidden = sb("hidden", [P, HC, P])
        row_slots = sb("row_slots", [P, SLOTS, J], I32)
        normed = sb("normed", [P, 2, D])
        normed_t = sb("normed_t", [P, 2, KC, P])
        x1 = sb("x1", [P, D])
        y_biased = sb("y_biased", [P, D])
        stats = sb("stats", [P, 2, 6])
        moments = sb("moments", [P, 2, 2])
        deviation = sb("deviation", [P, 2, 1])
        rstd = sb("rstd", [P, 2, 1])
        eps = sb("eps", [P, 1])
        ident = sb("ident", [P, P])
        ones = sb("ones", [P, P])
        before = sb("before", [P, P])
        iota1 = sb("iota1", [P, P])
        part = sb("part", [P, 1])
        block_first = sb("block_first", [P, NB])
        low_mask = sb("low_mask", [P, NGP])
        high_mask = sb("high_mask", [P, NGP])
        gmin = sb("gmin", [P, GT])
        gmax = sb("gmax", [P, GT])
        fits = sb("fits", [P, GT])
        wide = sb("wide", [P, GT])
        gmin_i = sb("gmin_i", [P, NGP], I32)
        gtmp_i = sb("gtmp_i", [P, NGP], I32)
        first_block = sb("first_block", [P, NGP], I32)
        any_wide = sb("any_wide", [P, 1])
        flag_i = sb("flag_i", [1, 1], I32)
        bias_b = sb("bias_b", [P, D])
        b2_b = sb("b2_b", [P, D])
        wr_b = sb("wr_b", [P, D])
        br_b = sb("br_b", [P, 1])
        b1_col = sb("b1_col", [P, HC])
        w_block = sb("w_block", [P, 2])
        w_all = sb("w_all", [P, NB])
        shifted = sb("shifted", [P, J])

        pick_counts = sb("pick_counts", [P, 15])
        above_count = sb("above_count", [P, 1])
        tied = sb("tied", [P, NB])
        above = sb("above", [P, NB])
        digits = sb("digits", [P, 15])
        candidates = sb("candidates", [P, 15])
        reached = sb("reached", [P, 15])
        floor_ = sb("floor_", [P, 1])
        passed = sb("passed", [P, 1])
        compared = sb("compared", [P, 15, NB])
        key_hi = sb("key_hi", [P, NB])
        key_lo = sb("key_lo", [P, NB])
        key_i = sb("key_i", [P, NB], I32)
        sign_i = sb("sign_i", [P, NB], I32)
        half_i = sb("half_i", [P, NB], I32)
        tie_base = sb("tie_base", [P, NB + 1])
        zeros = sb("zeros", [P, NB])
        quota = sb("quota", [P, 1])
        keep = sb("keep", [P, NB])
        real = sb("real", [P, 1])
        pad_key = sb("pad_key", [P, 1])

        banks = [ctx.enter_context(nc.psum_tensor(f"bank{i}", [P, BANK], F32)) for i in range(8)]

        edges_in = [sem(f"edges_in{i}") for i in range(3)]
        pads_set = sem("pads_set")
        node_pad_set = sem("node_pad_set")
        x_in = [sem(f"x_in{i}") for i in range(2)]
        x_last_in = sem("x_last_in")
        rel_in = sem("rel_in")
        small_in = sem("small_in")
        ffn_w_in = sem("ffn_w_in")
        consts = sem("consts")
        index_step = sem("index_step")
        rows_made = sem("rows_made")
        keys_made = sem("keys_made")
        turned = sem("turned")
        turned_by_act = sem("turned_by_act")
        turned_by_dve = sem("turned_by_dve")
        spread = sem("spread")
        norm_step = sem("norm_step")
        norm_deviation = sem("norm_deviation")
        norm_ready = sem("norm_ready")
        norm_turned = sem("norm_turned")
        norm_t_ready = sem("norm_t_ready")
        product_ready = sem("product_ready")
        bank_free = [sem(f"bank_free{i}") for i in range(5)]
        stored = [sem(f"stored{i}") for i in range(2)]
        last_stored = sem("last_stored")
        tables_ready = sem("tables_ready")
        rows_ready = [sem(f"rows_ready{i}") for i in range(SLOTS)]
        gathered = [sem(f"gathered{i}") for i in range(SLOTS)]
        onehot_ready = [sem(f"onehot_ready{i}") for i in range(SLOTS)]
        group_summed = [sem(f"group_summed{i}") for i in range(SLOTS)]
        sum_taken = [sem(f"sum_taken{i}") for i in range(SLOTS)]
        wide_rows = sem("wide_rows")
        wide_gathered = sem("wide_gathered")
        wide_group_done = sem("wide_group_done")
        wide_step = sem("wide_step")
        wide_onehot = sem("wide_onehot")
        wide_summed = sem("wide_summed")
        wide_added = sem("wide_added")
        wait_carrier = sem("wait_carrier")
        pool_carrier = sem("pool_carrier")
        ffn_step = sem("ffn_step")
        ffn_deviation = sem("ffn_deviation")
        ffn_norm = sem("ffn_norm")
        ffn_turned = sem("ffn_turned")
        ffn_norm_t = sem("ffn_norm_t")
        ffn_up = sem("ffn_up")
        ffn_gelu = sem("ffn_gelu")
        ffn_down = sem("ffn_down")
        ffn_done = sem("ffn_done")
        pick_step = sem("pick_step")
        counts_in = sem("counts_in")
        counts_out = sem("counts_out")
        output_ready = sem("output_ready")
        written = sem("written")

        ready_f = sb("ready_f", [1, P])
        ready_rev = sb("ready_rev", [1, P])
        done_f = sb("done_f", [1, P])
        done_before = sb("done_before", [1, P + 1], I32)
        one_row = sb("one_row", [1, P])
        first_block_f = sb("first_block_f", [1, NGP])

        block = ctx.enter_context(nc.Block())

        @block.sync
        def _(sp):
            sp.wait_ge(pads_set, 3)
            full_tiles = NG_FULL // P
            rest = NG_FULL - full_tiles * P
            for k, (a, to) in enumerate(((src, src_nat), (edge_type, type_nat), (dst, dst_nat))):
                to3 = to.rearrange("p (t e) -> p t e", e=GE)
                sp.dma_start(to3[:, 0:full_tiles, :],
                             a[0:full_tiles * P * GE].rearrange("(t p e) -> p t e", p=P, e=GE)).then_inc(edges_in[k], 16)
                sp.dma_start(to3[0:rest, full_tiles, :],
                             a[full_tiles * P * GE:NG_FULL * GE].rearrange("(p e) -> p e", e=GE)).then_inc(edges_in[k], 16)
                sp.dma_start(to3[rest:rest + 1, full_tiles, 0:E - NG_FULL * GE],
                             a[NG_FULL * GE:E].rearrange("(p e) -> p e", p=1)).then_inc(edges_in[k], 16)
            for k in range(KC):
                sp.dma_start(rel_sb[:, k, 0:TW].rearrange("p (r o) -> p r o", r=R),
                             rel_w[:, k * P:(k + 1) * P, :].rearrange("r p o -> p r o")).then_inc(rel_in, 16)
                sp.dma_start(rel_sb[:, k, TW:TW + D], loop_w[k * P:(k + 1) * P, :]).then_inc(rel_in, 16)
            for to, a in ((bias_b, h_bias), (b2_b, b2)):
                sp.dma_start(to[:, :], a.rearrange("(o d) -> o d", o=1).broadcast_to([P, D])).then_inc(small_in, 16)
            sp.dma_start(wr_b[:, :], wr.rearrange("d o -> o d").broadcast_to([P, D])).then_inc(small_in, 16)
            sp.dma_start(br_b[:, :], br.rearrange("(o d) -> o d", o=1).broadcast_to([P, 1])).then_inc(small_in, 16)
            sp.dma_start(b1_col[:, :], b1.rearrange("(m p) -> p m", p=P),
                         allow_slow_non_contiguous=True).then_inc(small_in, 16)
            with sp.Fori(0, NB // 2) as i:
                for u in range(2):
                    for k in range(4):
                        sp.wait_ge(bank_free[k], 2 * i + u + 1)
                    sp.dma_start(table_blocks[2 * i + u], stage[:, u, :]).then_inc(stored[u], 16)
            for k in range(4):
                sp.wait_ge(bank_free[k], NB)
            sp.dma_start(table_blocks[NB - 1], stage[:, 0, :]).then_inc(last_stored, 16)
            sp.wait_ge(product_ready, 5 * NB)
            sp.dma_start(w1_sb, w1.rearrange("(k p) h -> p k h", p=P)).then_inc(ffn_w_in, 16)
            sp.dma_start(w2_sb, w2.rearrange("(m p) d -> p m d", p=P)).then_inc(ffn_w_in, 16)
            with sp.Fori(0, NB - 1) as b:
                sp.wait_ge(output_ready, b + 1)
                sp.dma_start(out[0:(NB - 1) * P, :].rearrange("(b p) d -> b p d", p=P)[b], nodes[:, b, :]).then_inc(written, 16)
            sp.wait_ge(output_ready, NB)
            sp.dma_start(out[(NB - 1) * P:N, :], nodes[0:LAST, NB - 1, :]).then_inc(written, 16)
            sp.wait_ge(written, 16 * NB)

        @block.gpsimd
        def _(pool):
            nc.gpsimd.memset(src_nat[:, 3 * GE:SL], 0).then_inc(pads_set, 1)
            nc.gpsimd.memset(type_nat[:, 3 * GE:SL], 0).then_inc(pads_set, 1)
            nc.gpsimd.memset(dst_nat[:, 3 * GE:SL], -1).then_inc(pads_set, 1)
            nc.gpsimd.memset(nodes[:, NB - 1, :], 0.0).then_inc(node_pad_set, 1)
            nc.gpsimd.memset(ident[:, :], 0.0).then_inc(node_pad_set, 1)
            nc.gpsimd.memset(before[:, :], 1.0).then_inc(node_pad_set, 1)
            nc.gpsimd.memset(ones[:, :], 1.0).then_inc(consts, 1)
            nc.gpsimd.memset(eps[:, :], EPS).then_inc(consts, 1)
            nc.gpsimd.iota(iota1[:, :], [[1, P]], base=1, channel_multiplier=0,
                           allow_small_or_imprecise_dtypes=True).then_inc(consts, 1)
            nc.gpsimd.iota(part[:, :], [[0, 1]], base=0, channel_multiplier=1,
                           allow_small_or_imprecise_dtypes=True).then_inc(consts, 1)
            nc.gpsimd.iota(block_first[:, :], [[P, NB]], base=0, channel_multiplier=0,
                           allow_small_or_imprecise_dtypes=True).then_inc(consts, 1)
            pool.wait_ge(node_pad_set, 3)
            nc.gpsimd.affine_select(out=ident[:, :], in_=ident[:, :], compare_op=ALU.not_equal, fill=1.0,
                                    base=0, pattern=[[-1, P]], channel_multiplier=1).then_inc(consts, 1)
            nc.gpsimd.affine_select(out=before[:, :], in_=before[:, :], compare_op=ALU.is_gt, fill=0.0,
                                    base=0, pattern=[[1, P]], channel_multiplier=-1).then_inc(consts, 1)
            pool.dma_start(nodes[0:LAST, NB - 1, :], x[(NB - 1) * P:N, :]).then_inc(x_last_in, 16)
            x_blocks = x[0:(NB - 1) * P, :].rearrange("(b p) d -> b p d", p=P)
            with pool.Fori(0, NB // 2) as i:
                for u in range(2):
                    pool.wait_ge(x_in[u], 16 * i)
                    pool.dma_start(nodes[:, 2 * i + u, :], x_blocks[2 * i + u]).then_inc(x_in[u], 16)
            for u in range(2):
                pool.wait_ge(stored[u], 16 * (NB // 2))
            pool.wait_ge(last_stored, 16)
            last_row = pool.to_reg(NB * P * R - 1)
            with pool.Fori(0, ROUNDS) as i:
                for u in range(SLOTS):
                    pool.wait_ge(rows_ready[u], i + 1)
                    pool.wait_ge(group_summed[u], i)
                    pool.sem_inc(pool_carrier, 1)
                    for j in range(J):
                        pool.indirect_dma_start(messages[:, u, j * D:(j + 1) * D], None, table,
                                                bass.IndirectOffsetOnAxis(ap=row_slots[:, u, j:j + 1], axis=0),
                                                bounds_check=last_row).then_inc(gathered[u], 16)
            pool.wait_ge(tables_ready, 2)
            wide_flag = pool.value_load(flag_i[0:1, 0:1], min_val=0, max_val=1)
            with pool.If(wide_flag > 0):
                with pool.Fori(0, NG) as g:
                    pool.wait_ge(wide_rows, g + 1)
                    pool.sem_inc(pool_carrier, 1)
                    for j in range(J):
                        pool.indirect_dma_start(messages[:, 0, j * D:(j + 1) * D], None, table,
                                                bass.IndirectOffsetOnAxis(ap=row_slots[:, 0, j:j + 1], axis=0),
                                                bounds_check=last_row).then_inc(wide_gathered, 16)

        @block.scalar
        def _(act):
            for t in range(GT):
                act.wait_ge(turned, t + 1)
                nc.scalar.activation(gather_rows[:, t * P:(t + 1) * P, :].rearrange("p g j -> p j g"),
                                     banks[t][:, :].rearrange("p (j g) -> p j g", j=J), ACT.Copy).then_inc(turned_by_act, 1)

            def deviate(b, u):
                act.wait_ge(norm_step, 3 * b + 2)
                nc.scalar.activation(deviation[:, u, :], moments[:, u, 1:2], ACT.Sqrt, bias=eps[:, 0:1]).then_inc(norm_deviation, 1)

            def turn(b, u):
                act.wait_ge(norm_turned, b + 1)
                if not isinstance(b, int) or b > 1:
                    act.wait_ge(product_ready, 5 * (b - 1))
                nc.scalar.activation(normed_t[:, u, :, :].rearrange("p k n -> p (k n)"), banks[5 + u][:, 0:D],
                                     ACT.Copy).then_inc(norm_t_ready, 1)

            def evacuate(b, u, turn_no):
                act.wait_ge(stored[u], 16 * turn_no)
                for k in range(2):
                    act.wait_ge(product_ready, 5 * b + k + 1)
                    nc.scalar.activation(stage[:, u, k * BANK:(k + 1) * BANK], banks[k][:, :], ACT.Copy)\
                        .then_inc(bank_free[k], 1)

            act.wait_ge(consts, 7)
            deviate(0, 0)
            turn(0, 0)
            with act.Fori(0, NB // 2) as i:
                for u in range(2):
                    b = 2 * i + u
                    deviate(b + 1, 1 - u)
                    turn(b + 1, 1 - u)
                    evacuate(b, u, i)
            evacuate(NB - 1, 0, NB // 2)

            act.wait_ge(turned_by_act, GT)
            with act.Fori(0, ROUNDS) as i:
                for u in range(SLOTS):
                    act.wait_ge(gathered[u], 64 * i)
                    nc.scalar.activation(row_slots[:, u, :], gather_rows[:, SLOTS * i + u, :], ACT.Copy).then_inc(rows_ready[u], 1)
            act.wait_ge(tables_ready, 2)
            wide_flag = act.value_load(flag_i[0:1, 0:1], min_val=0, max_val=1)
            with act.If(wide_flag > 0):
                act.wait_ge(group_summed[0], ROUNDS)
                with act.Fori(0, NG) as g:
                    act.wait_ge(wide_group_done, g)
                    nc.scalar.activation(row_slots[:, 0, :], gather_rows[:, g, :], ACT.Copy).then_inc(wide_rows, 1)

            act.wait_ge(small_in, 16 * 5)
            with act.Fori(0, NB) as b:
                act.wait_ge(ffn_step, 8 * b + 4)
                nc.scalar.activation(deviation[:, 0, :], moments[:, 0, 1:2], ACT.Sqrt, bias=eps[:, 0:1]).then_inc(ffn_deviation, 1)
                act.wait_ge(ffn_turned, b + 1)
                act.wait_ge(ffn_up, b)
                nc.scalar.activation(normed_t[:, 0, :, :].rearrange("p k n -> p (k n)"), banks[4][:, 0:D],
                                     ACT.Copy).then_inc(ffn_norm_t, 1)
                act.wait_ge(ffn_up, b + 1)
                act.wait_ge(ffn_down, b)
                for m in range(HC):
                    last = nc.scalar.activation(hidden[:, m, :], banks[5 + m // 4][:, m % 4 * P:(m % 4 + 1) * P],
                                                ACT.Gelu_apprx_tanh, bias=b1_col[:, m:m + 1])
                last.then_inc(ffn_gelu, 1)

        @block.tensor
        def _(pe):
            pe.wait_ge(consts, 7)
            for k, (table_nat, made) in enumerate(((row_nat, 1), (key_nat, 2), (dst_f, 3))):
                if k == 0:
                    pe.wait_ge(rows_made, 1)
                else:
                    pe.wait_ge(keys_made, k)
                for t in range(GT):
                    n = k * GT + t
                    if k == 1:
                        pe.wait_ge(turned_by_act, t + 1)
                    if k == 2:
                        pe.wait_ge(turned_by_dve, t + 1)
                    for j in range(J):
                        last = nc.tensor.transpose(banks[t][:, j * P:(j + 1) * P],
                                                   table_nat[:, t * GE + j * P:t * GE + (j + 1) * P], ident[:, :])
                    last.then_inc(turned, 1)
            for t in range(GT):
                last = nc.tensor.matmul(banks[4][:, t * P:(t + 1) * P], gmin[:, t:t + 1].broadcast_to([P, P]),
                                        ident[:, :], start=True, stop=True)
            nc.tensor.matmul(banks[5][:, 0:GT], ones[:, :], wide[:, :], start=True, stop=True).then_inc(spread, 1)

            def turn(b, u):
                pe.wait_ge(norm_ready, b + 1)
                for k in range(KC):
                    last = nc.tensor.transpose(banks[5 + u][:, k * P:(k + 1) * P], normed[:, u, k * P:(k + 1) * P], ident[:, :])
                last.then_inc(norm_turned, 1)

            def products(b, u):
                pe.wait_ge(norm_t_ready, b + 1)
                for n in range(5):
                    width = BANK if n < 4 else D
                    pe.wait_ge(bank_free[n], b)
                    for k in range(KC):
                        last = nc.tensor.matmul(banks[n][:, 0:width], normed_t[:, u, k, :],
                                                rel_sb[:, k, n * BANK:n * BANK + width], start=(k == 0), stop=(k == KC - 1))
                    last.then_inc(product_ready, 1)

            pe.wait_ge(turned_by_dve, 2 * GT + 1)
            turn(0, 0)
            pe.wait_ge(rel_in, 16 * 2 * KC)
            with pe.Fori(0, NB // 2) as i:
                for u in range(2):
                    b = 2 * i + u
                    turn(b + 1, 1 - u)
                    products(b, u)
            products(NB - 1, 0)

            for n in range(5):
                pe.wait_ge(bank_free[n], NB)
            with pe.Fori(0, ROUNDS) as i:
                for u in range(SLOTS):
                    pe.wait_ge(onehot_ready[u], i + 1)
                    pe.wait_ge(gathered[u], 64 * (i + 1))
                    pe.wait_ge(sum_taken[u], 2 * i)
                    for j in range(J):
                        last = nc.tensor.matmul(banks[u][:, 0:D], onehot[:, u, j, :], messages[:, u, j * D:(j + 1) * D],
                                                start=(j == 0), stop=(j == J - 1))
                    last.then_inc(group_summed[u], 1)

            wide_flag = pe.value_load(flag_i[0:1, 0:1], min_val=0, max_val=1)
            with pe.If(wide_flag > 0):
                with pe.Fori(0, NG) as g:
                    with pe.Fori(0, NB) as b:
                        pe.wait_ge(wide_gathered, 64 * (g + 1))
                        pe.wait_ge(wide_onehot, g * NB + b + 1)
                        pe.wait_ge(wide_added, g * NB + b)
                        for j in range(J):
                            last = nc.tensor.matmul(banks[0][:, 0:D], onehot[:, 0, j, :], messages[:, 0, j * D:(j + 1) * D],
                                                    start=(j == 0), stop=(j == J - 1))
                        last.then_inc(wide_summed, 1)
                    pe.nop().then_inc(wide_group_done, 1)

            pe.wait_ge(ffn_w_in, 32)
            with pe.Fori(0, NB) as b:
                pe.wait_ge(ffn_norm, b + 1)
                for k in range(KC):
                    last = nc.tensor.transpose(banks[4][:, k * P:(k + 1) * P], normed[:, 0, k * P:(k + 1) * P], ident[:, :])
                last.then_inc(ffn_turned, 1)
                pe.wait_ge(ffn_norm_t, b + 1)
                for m in range(HC):
                    for k in range(KC):
                        last = nc.tensor.matmul(banks[5 + m // 4][:, m % 4 * P:(m % 4 + 1) * P],
                                                w1_sb[:, k, m * P:(m + 1) * P], normed_t[:, 0, k, :],
                                                start=(k == 0), stop=(k == KC - 1))
                last.then_inc(ffn_up, 1)
                pe.wait_ge(ffn_gelu, b + 1)
                for m in range(HC):
                    last = nc.tensor.matmul(banks[7][:, 0:D], hidden[:, m, :], w2_sb[:, m, :],
                                            start=(m == 0), stop=(m == HC - 1))
                last.then_inc(ffn_down, 1)

            for r in range(8):
                pe.wait_ge(counts_in, r + 1)
                nc.tensor.matmul(banks[0][:, 0:15], ones[:, :], pick_counts[:, :], start=True, stop=True).then_inc(counts_out, 1)
            pe.wait_ge(counts_in, 9)
            nc.tensor.matmul(banks[0][:, 0:1], ones[:, :], above_count[:, :], start=True, stop=True)
            nc.tensor.matmul(banks[1][:, 0:NB], ones[:, :], tied[:, :], start=True, stop=True)
            nc.tensor.matmul(banks[2][:, 0:NB], before[:, :], tied[:, :], start=True, stop=True).then_inc(counts_out, 1)

        @block.vector
        def _(dve):
            V = nc.vector
            count = {}

            def link(s, ins):
                count[s.name] = count.get(s.name, 0) + 1
                ins.then_inc(s, 1)
                dve.wait_ge(s, count[s.name])

            for k in range(3):
                dve.wait_ge(edges_in[k], 48)
            V.scalar_tensor_tensor(row_nat, src_nat, float(R), type_nat, ALU.mult, ALU.add).then_inc(rows_made, 1)
            link(index_step, V.tensor_copy(dst_f, dst_nat))
            link(index_step, V.tensor_scalar(key_nat, dst_f, 0.0, 16384.0, ALU.is_lt, ALU.mult))
            link(index_step, V.tensor_tensor(key_nat, key_nat, dst_f, ALU.add))
            link(index_step, V.tensor_reduce(gmin[:, :], key_nat.rearrange("p (t e) -> p t e", e=GE), AX.X, ALU.min))
            link(index_step, V.tensor_reduce(gmax[:, :], dst_f.rearrange("p (t e) -> p t e", e=GE), AX.X, ALU.max))
            link(index_step, V.tensor_scalar_min(gmin[:, :], gmin[:, :], float(N - 1)))
            link(index_step, V.tensor_tensor(fits[:, :], gmax[:, :], gmin[:, :], ALU.subtract))
            link(index_step, V.tensor_scalar(wide[:, :], fits[:, :], float(P), None, ALU.is_ge))
            link(index_step, V.tensor_scalar(fits[:, :], wide[:, :], -1.0, 1.0, ALU.mult, ALU.add))
            dve.wait_ge(rows_made, 1)
            link(index_step, V.tensor_scalar(masked_i, dst_nat, P - 1, None, ALU.bitwise_and))
            link(index_step, V.tensor_scalar(key_nat, masked_i, 1.0, None, ALU.add))
            for t in range(GT):
                part_of = slice(t * GE, (t + 1) * GE)
                link(index_step, V.tensor_scalar(valid_f[:, part_of], dst_f[:, part_of], 0.0, fits[:, t:t + 1], ALU.is_ge, ALU.mult))
            V.tensor_tensor(key_nat, key_nat, valid_f, ALU.mult).then_inc(keys_made, 1)
            for t in range(GT):
                part_of = slice(t * GE, (t + 1) * GE)
                last = V.tensor_scalar(dst_f[:, part_of], dst_f[:, part_of], 1.0, wide[:, t:t + 1], ALU.add, ALU.mult)
            last.then_inc(keys_made, 1)
            for k, to in enumerate((window_keys, wide_keys)):
                for t in range(GT):
                    dve.wait_ge(turned, (k + 1) * GT + t + 1)
                    V.tensor_copy(to[:, t * P:(t + 1) * P, :].rearrange("p g j -> p j g"),
                                  banks[t][:, :].rearrange("p (j g) -> p j g", j=J)).then_inc(turned_by_dve, 1)
            dve.wait_ge(spread, 1)
            link(index_step, V.tensor_copy(gmin_i[:, :], banks[4][:, :]))
            link(index_step, V.tensor_reduce(any_wide[:, :], banks[5][:, 0:GT], AX.X, ALU.max))
            link(index_step, V.tensor_scalar_min(any_wide[:, :], any_wide[:, :], 1.0))
            V.tensor_copy(flag_i[:, :], any_wide[0:1, :]).then_inc(turned_by_dve, 1)
            link(index_step, V.tensor_scalar(gtmp_i[:, :], gmin_i[:, :], P - 1, None, ALU.bitwise_and))
            link(index_step, V.tensor_scalar(low_mask[:, :], gtmp_i[:, :], part[:, 0:1], None, ALU.is_le))
            link(index_step, V.tensor_scalar(high_mask[:, :], low_mask[:, :], -1.0, 1.0, ALU.mult, ALU.add))
            link(index_step, V.tensor_scalar(first_block[:, :], gmin_i[:, :], 7, None, ALU.logical_shift_right))
            V.memset(zeros[:, :], 0.0)
            V.memset(acc[:, NB, :], 0.0).then_inc(tables_ready, 1)
            dve.wait_ge(turned_by_dve, 2 * GT + 1)
            V.nop().then_inc(tables_ready, 1)

            NORM_STEPS = 3

            def norm(b, u):
                V.bn_stats(stats[:, u, :], nodes[:, b, :]).then_inc(norm_step, 1)
                dve.wait_ge(norm_step, NORM_STEPS * b + 1)
                dve.sem_inc(wait_carrier, 1)
                V.bn_aggr(moments[:, u, :], stats[:, u, :]).then_inc(norm_step, 1)
                dve.wait_ge(norm_deviation, b + 1)
                V.reciprocal(rstd[:, u, :], deviation[:, u, :]).then_inc(norm_step, 1)
                dve.wait_ge(norm_step, NORM_STEPS * b + 3)
                if not isinstance(b, int) or b > 1:
                    dve.wait_ge(norm_turned, b - 1)
                V.tensor_scalar(normed[:, u, :], nodes[:, b, :], moments[:, u, 0:1], rstd[:, u, 0:1],
                                ALU.subtract, ALU.mult).then_inc(norm_ready, 1)

            def evacuate(b, u):
                for k in (2, 3):
                    dve.wait_ge(product_ready, 5 * b + k + 1)
                    V.tensor_copy(stage[:, u, k * BANK:(k + 1) * BANK], banks[k][:, :])\
                        .then_inc(bank_free[k], 1)
                dve.wait_ge(product_ready, 5 * b + 5)
                V.tensor_copy(acc[:, b, :], banks[4][:, 0:D]).then_inc(bank_free[4], 1)

            dve.wait_ge(x_in[0], 16)
            norm(0, 0)
            with dve.Fori(0, NB // 2 - 1) as i:
                dve.wait_ge(x_in[1], 16 * (i + 1))
                norm(2 * i + 1, 1)
                dve.wait_ge(stored[0], 16 * i)
                evacuate(2 * i, 0)
                dve.wait_ge(x_in[0], 16 * (i + 2))
                norm(2 * i + 2, 0)
                dve.wait_ge(stored[1], 16 * i)
                evacuate(2 * i + 1, 1)
            i = NB // 2 - 1
            dve.wait_ge(x_in[1], 16 * (i + 1))
            norm(2 * i + 1, 1)
            dve.wait_ge(stored[0], 16 * i)
            evacuate(2 * i, 0)
            dve.wait_ge(x_last_in, 16)
            norm(NB - 1, 0)
            dve.wait_ge(stored[1], 16 * i)
            evacuate(2 * i + 1, 1)
            dve.wait_ge(stored[0], 16 * (NB // 2))
            evacuate(NB - 1, 0)

            def build(g, u, turn_no):
                dve.wait_ge(group_summed[u], turn_no)
                for j in range(J):
                    last = V.tensor_scalar(onehot[:, u, j, :], iota1[:, :], window_keys[:, g, j:j + 1], None, ALU.is_equal)
                last.then_inc(onehot_ready[u], 1)

            dve.wait_ge(turned_by_dve, 2 * GT + 1)
            dve.wait_ge(bank_free[4], NB)
            build(0, 0, 0)
            build(1, 1, 0)
            with dve.Fori(0, ROUNDS) as i:
                for u in range(SLOTS):
                    g = SLOTS * i + u
                    build(g + 2, (u + 2) % SLOTS, i + (u + 2) // SLOTS)
                    b0 = dve.value_load(first_block[0:1, bass.ds(g, 1)], min_val=0, max_val=NB - 1)
                    dve.wait_ge(group_summed[u], i + 1)
                    dve.wait_ge(sum_taken[(u - 1) % SLOTS], 2 * (i + 1) if u else 2 * i)
                    for k, mask in enumerate((low_mask, high_mask)):
                        V.scalar_tensor_tensor(acc[:, b0 + k, :], banks[u][:, 0:D], mask[:, bass.ds(g, 1)], acc[:, b0 + k, :],
                                               ALU.mult, ALU.add).then_inc(sum_taken[u], 1)
            dve.wait_ge(sum_taken[SLOTS - 1], 2 * ROUNDS)

            wide_flag = dve.value_load(flag_i[0:1, 0:1], min_val=0, max_val=1)
            with dve.If(wide_flag > 0):
                with dve.Fori(0, NG) as g:
                    with dve.Fori(0, NB) as b:
                        n = g * NB + b
                        V.tensor_scalar(shifted[:, :], wide_keys[:, g, :], block_first[:, bass.ds(b, 1)], None,
                                        ALU.subtract).then_inc(wide_step, 1)
                        dve.wait_ge(wide_step, n + 1)
                        for j in range(J):
                            last = V.tensor_scalar(onehot[:, 0, j, :], iota1[:, :], shifted[:, j:j + 1], None, ALU.is_equal)
                        last.then_inc(wide_onehot, 1)
                        dve.wait_ge(wide_summed, n + 1)
                        V.tensor_tensor(acc[:, b, :], banks[0][:, 0:D], acc[:, b, :], ALU.add).then_inc(wide_added, 1)
                dve.wait_ge(wide_added, NG * NB)

            dve.wait_ge(small_in, 16 * 5)
            FS = 8
            with dve.Fori(0, NB) as b:
                def step(n, ins):
                    ins.then_inc(ffn_step, 1)
                    dve.wait_ge(ffn_step, FS * b + n)
                step(1, V.scalar_tensor_tensor(x1[:, :], acc[:, b, :], SCALE, nodes[:, b, :], ALU.mult, ALU.add))
                step(2, V.tensor_tensor(x1[:, :], x1[:, :], bias_b[:, :], ALU.add))
                V.bn_stats(stats[:, 0, :], x1[:, :]).then_inc(ffn_step, 1)
                dve.wait_ge(ffn_step, FS * b + 3)
                dve.sem_inc(wait_carrier, 1)
                step(4, V.bn_aggr(moments[:, 0, :], stats[:, 0, :]))
                dve.wait_ge(ffn_deviation, b + 1)
                step(5, V.reciprocal(rstd[:, 0, :], deviation[:, 0, :]))
                dve.wait_ge(ffn_turned, b)
                V.tensor_scalar(normed[:, 0, :], x1[:, :], moments[:, 0, 0:1], rstd[:, 0, 0:1],
                                ALU.subtract, ALU.mult).then_inc(ffn_norm, 1)
                dve.wait_ge(ffn_norm, b + 1)
                step(6, V.tensor_tensor(nodes[:, b, :], x1[:, :], normed[:, 0, :], ALU.add))
                step(7, V.tensor_tensor_reduce(out=y_biased[:, :], in0=normed[:, 0, :], in1=wr_b[:, :], scale=1.0, scalar=0.0,
                                               op0=ALU.mult, op1=ALU.add, accum_out=w_block[:, 0:1]))
                V.tensor_scalar(w_block[:, 1:2], w_block[:, 0:1], br_b[:, 0:1], None, ALU.add)
                step(8, V.tensor_scalar(w_all[:, bass.ds(b, 1)], w_block[:, 0:1], br_b[:, 0:1], None, ALU.add))
                dve.wait_ge(ffn_down, b + 1)
                V.tensor_tensor(y_biased[:, :], banks[7][:, 0:D], b2_b[:, :], ALU.add).then_inc(ffn_done, 1)
                dve.wait_ge(ffn_done, 2 * b + 1)
                V.tensor_scalar(acc[:, b, :], y_biased[:, :], w_block[:, 1:2], None, ALU.mult).then_inc(ffn_done, 1)
                dve.wait_ge(ffn_done, 2 * b + 2)

            w_bits = w_all[:, :].bitcast(I32)
            link(pick_step, V.tensor_scalar(sign_i[:, :], w_bits, 31, 0x7FFFFFFF, ALU.arith_shift_right, ALU.bitwise_and))
            link(pick_step, V.tensor_tensor(key_i[:, :], w_bits, sign_i[:, :], ALU.bitwise_xor))
            link(pick_step, V.tensor_scalar(half_i[:, :], key_i[:, :], 16, None, ALU.arith_shift_right))
            link(pick_step, V.tensor_copy(key_hi[:, :], half_i[:, :]))
            link(pick_step, V.tensor_scalar(half_i[:, :], key_i[:, :], 0xFFFF, None, ALU.bitwise_and))
            link(pick_step, V.tensor_copy(key_lo[:, :], half_i[:, :]))
            link(pick_step, V.tensor_scalar(real[:, :], part[:, :], float(LAST), None, ALU.is_lt))
            link(pick_step, V.tensor_scalar(pad_key[:, :], real[:, :], 40000.0, -40000.0, ALU.mult, ALU.add))
            link(pick_step, V.tensor_scalar(key_hi[:, NB - 1:NB], key_hi[:, NB - 1:NB], real[:, 0:1], pad_key[:, 0:1], ALU.mult, ALU.add))
            link(pick_step, V.tensor_scalar(digits[:, :], iota1[:, 0:15], 1.0, None, ALU.mult))

            def radix_round(r, keys, shift):
                link(pick_step, V.tensor_scalar(candidates[:, :], digits[:, :], float(1 << shift), floor_[:, 0:1], ALU.mult, ALU.add))
                link(pick_step, V.tensor_tensor(compared[:, :, :], keys.unsqueeze(1).broadcast_to([P, 15, NB]),
                                                candidates[:, :].unsqueeze(2).broadcast_to([P, 15, NB]), ALU.is_ge))
                V.tensor_reduce(pick_counts[:, :], compared[:, :, :], AX.X, ALU.add).then_inc(counts_in, 1)
                dve.wait_ge(counts_out, r + 1)
                link(pick_step, V.tensor_scalar(reached[:, :], banks[0][:, 0:15], float(SELECTED), None, ALU.is_ge))
                link(pick_step, V.tensor_reduce(passed[:, :], reached[:, :], AX.X, ALU.add))
                link(pick_step, V.scalar_tensor_tensor(floor_[:, :], passed[:, :], float(1 << shift), floor_[:, :], ALU.mult, ALU.add))

            link(pick_step, V.memset(floor_[:, :], -32768.0))
            for r in range(4):
                radix_round(r, key_hi[:, :], 12 - 4 * r)
            link(pick_step, V.tensor_scalar(above[:, :], key_hi[:, :], floor_[:, 0:1], 65536.0, ALU.is_gt, ALU.mult))
            link(pick_step, V.tensor_scalar(tied[:, :], key_hi[:, :], floor_[:, 0:1], None, ALU.is_equal))
            link(pick_step, V.tensor_scalar(key_lo[:, :], key_lo[:, :], 1.0, None, ALU.add))
            link(pick_step, V.tensor_tensor(key_lo[:, :], key_lo[:, :], tied[:, :], ALU.mult))
            link(pick_step, V.tensor_tensor(key_lo[:, :], key_lo[:, :], above[:, :], ALU.add))
            link(pick_step, V.tensor_scalar(key_lo[:, :], key_lo[:, :], -1.0, None, ALU.add))
            link(pick_step, V.memset(floor_[:, :], 0.0))
            for r in range(4):
                radix_round(4 + r, key_lo[:, :], 12 - 4 * r)
            link(pick_step, V.tensor_scalar(above[:, :], key_lo[:, :], floor_[:, 0:1], None, ALU.is_gt))
            link(pick_step, V.tensor_scalar(tied[:, :], key_lo[:, :], floor_[:, 0:1], None, ALU.is_equal))
            V.tensor_reduce(above_count[:, :], above[:, :], AX.X, ALU.add).then_inc(counts_in, 1)
            dve.wait_ge(counts_out, 9)
            link(pick_step, V.tensor_scalar(quota[:, :], banks[0][:, 0:1], -1.0, float(SELECTED), ALU.mult, ALU.add))
            link(pick_step, V.memset(tie_base[:, 0:1], 0.0))
            link(pick_step, V.tensor_copy(key_hi[:, :], banks[1][:, 0:NB]))
            link(pick_step, V.tensor_tensor_scan(tie_base[:, 1:NB + 1], key_hi[:, :], zeros[:, :], 0.0, ALU.add, ALU.add))
            link(pick_step, V.tensor_tensor(keep[:, :], banks[2][:, 0:NB], tie_base[:, 0:NB], ALU.add))
            link(pick_step, V.tensor_scalar(keep[:, :], keep[:, :], quota[:, 0:1], None, ALU.is_lt))
            link(pick_step, V.tensor_tensor(keep[:, :], keep[:, :], tied[:, :], ALU.mult))
            link(pick_step, V.tensor_tensor(keep[:, :], keep[:, :], above[:, :], ALU.add))

            with dve.Fori(0, NB) as b:
                V.scalar_tensor_tensor(nodes[:, b, :], acc[:, b, :], keep[:, bass.ds(b, 1)], nodes[:, b, :],
                                       ALU.mult, ALU.add).then_inc(output_ready, 1)


_NAMES = ["x", "src", "dst", "edge_type_8", "L0_gnn_weight", "L0_gnn_h_bias", "L0_gnn_loop_weight",
          "L0_ffn_wr", "L0_ffn_br", "L0_ffn_w1", "L0_ffn_b1", "L0_ffn_w2", "L0_ffn_b2"]


def kernel(**inputs):
    import numpy as _np
    import concourse.bacc as _bacc
    from concourse import mybir as _mybir
    from concourse.bass_utils import run_bass_kernel_spmd as _run

    nc = _bacc.Bacc("TRN2", target_bir_lowering=False, num_devices=1)
    arrays, args = {}, []
    for name in _NAMES:
        a = _np.ascontiguousarray(inputs[name])
        arrays[f"in_{name}"] = a
        args.append(nc.dram_tensor(f"in_{name}", a.shape, _mybir.dt.from_np(a.dtype), kind="ExternalInput").ap())
    shape = _np.shape(inputs["x"])
    args.append(nc.dram_tensor("node_out", shape, _mybir.dt.float32, kind="ExternalOutput").ap())
    gnn_ffn_program(nc, *args)
    r = _run(nc, [arrays], core_ids=[0])
    return r.results[0]["node_out"]
```

```python
import concourse.bass as bass
from concourse import mybir
from contextlib import ExitStack

P = 128
F32 = mybir.dt.float32
I32 = mybir.dt.int32
ALU = mybir.AluOpType
ACT = mybir.ActivationFunctionType
AX = mybir.AxisListType


def gnn_ffn_program(nc, x, src, dst, edge_type, rel_w, h_bias, loop_w, wr, br, w1, b1, w2, b2, out):
    N, D = x.shape
    E = src.shape[0]
    R = rel_w.shape[0]
    H = w1.shape[1]
    KC = D // P
    HC = H // P
    NB = -(-N // P)
    LAST = N - (NB - 1) * P
    J = 4
    GE = J * P
    SLOTS = 4
    NG_FULL = E // GE
    NG = -(-(-(-E // GE)) // SLOTS) * SLOTS
    ROUNDS = NG // SLOTS
    CONSTS = 7
    GT = 4
    NGP = GT * P
    assert NG + SLOTS <= NGP and NB % 2 == 1
    SELECTED = max(1, int(0.5 * N)) - 1
    SCALE = 0.7071067811865476
    EPS = 1e-5
    TW = R * D
    BANK = 512

    ctx = ExitStack()
    with ctx:
        def sb(name, shape, dt=F32):
            return ctx.enter_context(nc.sbuf_tensor(name, shape, dt))

        def sem(name):
            return ctx.enter_context(nc.semaphore(name))

        table = nc.dram_tensor("message_table", [NB * P * R, D], F32).ap()
        table_blocks = table.rearrange("(b p r) d -> b p (r d)", p=P, r=R)

        acc = sb("acc", [P, NB + 1, D])
        nodes = sb("nodes", [P, NB, D])
        messages = sb("messages", [P, SLOTS, J * D])
        weights = sb("weights", [P, KC * (TW + D)])
        gather_rows = sb("gather_rows", [P, NGP, J], I32)
        window_keys = sb("window_keys", [P, NGP, J])
        wide_keys = sb("wide_keys", [P, NGP, J])
        natural = acc[:, 0:48, :].rearrange("p b d -> p (b d)")
        SL = GT * GE

        def slab(k, dt=F32):
            return natural[:, k * SL:(k + 1) * SL].bitcast(dt) if dt is not F32 else natural[:, k * SL:(k + 1) * SL]

        src_nat, type_nat, dst_nat = (slab(k, I32) for k in range(3))
        row_nat, dst_f, key_nat = (slab(k) for k in (3, 4, 5))
        masked_i, valid_f, bit_f = slab(0, I32), slab(1), slab(0)
        stage = messages[:, :, :].rearrange("p s d -> p (s d)").rearrange("p (u c) -> p u c", u=2)
        rel_sb = weights[:, :].rearrange("p (k c) -> p k c", k=KC)
        w1_sb = weights[:, 0:KC * H].rearrange("p (k h) -> p k h", k=KC)
        w2_sb = weights[:, KC * H:KC * H + HC * D].rearrange("p (m d) -> p m d", m=HC)

        onehot = sb("onehot", [P, SLOTS, J, P])
        hidden = sb("hidden", [P, HC, P])
        row_slots = sb("row_slots", [P, SLOTS, J], I32)
        normed = sb("normed", [P, 2, D])
        normed_t = sb("normed_t", [P, 2, KC, P])
        x1 = sb("x1", [P, D])
        y_biased = sb("y_biased", [P, D])
        stats = sb("stats", [P, 2, 6])
        moments = sb("moments", [P, 2, 2])
        deviation = sb("deviation", [P, 2, 1])
        rstd = sb("rstd", [P, 2, 1])
        eps = sb("eps", [P, 1])
        ident = sb("ident", [P, P])
        ones = sb("ones", [P, P])
        before = sb("before", [P, P])
        iota1 = sb("iota1", [P, P])
        part = sb("part", [P, 1])
        block_first = sb("block_first", [P, NB])
        low_mask = sb("low_mask", [P, NGP])
        high_mask = sb("high_mask", [P, NGP])
        gmin = sb("gmin", [P, GT])
        gmax = sb("gmax", [P, GT])
        fits = sb("fits", [P, GT])
        wide = sb("wide", [P, GT])
        gmin_i = sb("gmin_i", [P, NGP], I32)
        gtmp_i = sb("gtmp_i", [P, NGP], I32)
        first_block = sb("first_block", [P, NGP], I32)
        any_wide = sb("any_wide", [P, 1])
        flag_i = sb("flag_i", [1, 1], I32)
        bias_b = sb("bias_b", [P, D])
        b2_b = sb("b2_b", [P, D])
        wr_b = sb("wr_b", [P, D])
        br_b = sb("br_b", [P, 1])
        b1_col = sb("b1_col", [P, HC])
        w_block = sb("w_block", [P, 2])
        w_all = sb("w_all", [P, NB])
        shifted = sb("shifted", [P, J])

        pick_counts = sb("pick_counts", [P, 15])
        above_count = sb("above_count", [P, 1])
        tied = sb("tied", [P, NB])
        above = sb("above", [P, NB])
        digits = sb("digits", [P, 15])
        candidates = sb("candidates", [P, 15])
        reached = sb("reached", [P, 15])
        floor_ = sb("floor_", [P, 1])
        passed = sb("passed", [P, 1])
        compared = sb("compared", [P, 15, NB])
        key_hi = sb("key_hi", [P, NB])
        key_lo = sb("key_lo", [P, NB])
        key_i = sb("key_i", [P, NB], I32)
        sign_i = sb("sign_i", [P, NB], I32)
        half_i = sb("half_i", [P, NB], I32)
        tie_base = sb("tie_base", [P, NB + 1])
        zeros = sb("zeros", [P, NB])
        quota = sb("quota", [P, 1])
        keep = sb("keep", [P, NB])
        real = sb("real", [P, 1])
        pad_key = sb("pad_key", [P, 1])

        banks = [ctx.enter_context(nc.psum_tensor(f"bank{i}", [P, BANK], F32)) for i in range(8)]

        edges_in = [sem(f"edges_in{i}") for i in range(3)]
        pads_set = sem("pads_set")
        node_pad_set = sem("node_pad_set")
        x_in = [sem(f"x_in{i}") for i in range(2)]
        x_last_in = sem("x_last_in")
        rel_in = sem("rel_in")
        small_in = sem("small_in")
        ffn_w_in = sem("ffn_w_in")
        consts = sem("consts")
        index_step = sem("index_step")
        rows_made = sem("rows_made")
        keys_made = sem("keys_made")
        turned = sem("turned")
        turned_by_act = sem("turned_by_act")
        turned_by_dve = sem("turned_by_dve")
        spread = sem("spread")
        norm_step = sem("norm_step")
        norm_deviation = sem("norm_deviation")
        norm_ready = sem("norm_ready")
        norm_turned = sem("norm_turned")
        norm_t_ready = sem("norm_t_ready")
        product_ready = sem("product_ready")
        bank_free = [sem(f"bank_free{i}") for i in range(5)]
        stored = [sem(f"stored{i}") for i in range(2)]
        last_stored = sem("last_stored")
        tables_ready = sem("tables_ready")
        rows_ready = [sem(f"rows_ready{i}") for i in range(SLOTS)]
        gathered = [sem(f"gathered{i}") for i in range(SLOTS)]
        onehot_ready = [sem(f"onehot_ready{i}") for i in range(SLOTS)]
        group_summed = [sem(f"group_summed{i}") for i in range(SLOTS)]
        sum_taken = [sem(f"sum_taken{i}") for i in range(SLOTS)]
        wide_rows = sem("wide_rows")
        wide_gathered = sem("wide_gathered")
        wide_group_done = sem("wide_group_done")
        wide_step = sem("wide_step")
        wide_onehot = sem("wide_onehot")
        wide_summed = sem("wide_summed")
        wide_added = sem("wide_added")
        wait_carrier = sem("wait_carrier")
        pool_carrier = sem("pool_carrier")
        ffn_step = sem("ffn_step")
        ffn_deviation = sem("ffn_deviation")
        ffn_norm = sem("ffn_norm")
        ffn_turned = sem("ffn_turned")
        ffn_norm_t = sem("ffn_norm_t")
        ffn_up = sem("ffn_up")
        ffn_gelu = sem("ffn_gelu")
        ffn_down = sem("ffn_down")
        ffn_done = sem("ffn_done")
        pick_step = sem("pick_step")
        counts_in = sem("counts_in")
        counts_out = sem("counts_out")
        output_ready = sem("output_ready")
        written = sem("written")

        ready = sb("ready", [1, 2, 2 * P])
        done_f = sb("done_f", [1, P])
        round_block = sb("round_block", [1, P + 1], I32)
        round_busy = sb("round_busy", [1, P], I32)
        left_over = sb("left_over", [1, NB], I32)
        block_no = sb("block_no", [1, NB])
        one_row = sb("one_row", [1, P])
        first_block_f = sb("first_block_f", [1, NGP])

        block = ctx.enter_context(nc.Block())

        @block.sync
        def _(sp):
            sp.wait_ge(pads_set, 3)
            full_tiles = NG_FULL // P
            rest = NG_FULL - full_tiles * P
            for k, (a, to) in enumerate(((src, src_nat), (edge_type, type_nat), (dst, dst_nat))):
                to3 = to.rearrange("p (t e) -> p t e", e=GE)
                sp.dma_start(to3[:, 0:full_tiles, :],
                             a[0:full_tiles * P * GE].rearrange("(t p e) -> p t e", p=P, e=GE)).then_inc(edges_in[k], 16)
                sp.dma_start(to3[0:rest, full_tiles, :],
                             a[full_tiles * P * GE:NG_FULL * GE].rearrange("(p e) -> p e", e=GE)).then_inc(edges_in[k], 16)
                sp.dma_start(to3[rest:rest + 1, full_tiles, 0:E - NG_FULL * GE],
                             a[NG_FULL * GE:E].rearrange("(p e) -> p e", p=1)).then_inc(edges_in[k], 16)
            for k in range(KC):
                sp.dma_start(rel_sb[:, k, 0:TW].rearrange("p (r o) -> p r o", r=R),
                             rel_w[:, k * P:(k + 1) * P, :].rearrange("r p o -> p r o")).then_inc(rel_in, 16)
                sp.dma_start(rel_sb[:, k, TW:TW + D], loop_w[k * P:(k + 1) * P, :]).then_inc(rel_in, 16)
            for to, a in ((bias_b, h_bias), (b2_b, b2)):
                sp.dma_start(to[:, :], a.rearrange("(o d) -> o d", o=1).broadcast_to([P, D])).then_inc(small_in, 16)
            sp.dma_start(wr_b[:, :], wr.rearrange("d o -> o d").broadcast_to([P, D])).then_inc(small_in, 16)
            sp.dma_start(br_b[:, :], br.rearrange("(o d) -> o d", o=1).broadcast_to([P, 1])).then_inc(small_in, 16)
            sp.dma_start(b1_col[:, :], b1.rearrange("(m p) -> p m", p=P),
                         allow_slow_non_contiguous=True).then_inc(small_in, 16)
            with sp.Fori(0, NB // 2) as i:
                for u in range(2):
                    for k in range(4):
                        sp.wait_ge(bank_free[k], 2 * i + u + 1)
                    sp.dma_start(table_blocks[2 * i + u], stage[:, u, :]).then_inc(stored[u], 16)
            for k in range(4):
                sp.wait_ge(bank_free[k], NB)
            sp.dma_start(table_blocks[NB - 1], stage[:, 0, :]).then_inc(last_stored, 16)
            sp.wait_ge(product_ready, 5 * NB)
            sp.dma_start(w1_sb, w1.rearrange("(k p) h -> p k h", p=P)).then_inc(ffn_w_in, 16)
            sp.dma_start(w2_sb, w2.rearrange("(m p) d -> p m d", p=P)).then_inc(ffn_w_in, 16)
            with sp.Fori(0, NB - 1) as b:
                sp.wait_ge(output_ready, b + 1)
                sp.dma_start(out[0:(NB - 1) * P, :].rearrange("(b p) d -> b p d", p=P)[b], nodes[:, b, :]).then_inc(written, 16)
            sp.wait_ge(output_ready, NB)
            sp.dma_start(out[(NB - 1) * P:N, :], nodes[0:LAST, NB - 1, :]).then_inc(written, 16)
            sp.wait_ge(written, 16 * NB)

        @block.gpsimd
        def _(pool):
            nc.gpsimd.memset(src_nat[:, 3 * GE:SL], 0).then_inc(pads_set, 1)
            nc.gpsimd.memset(type_nat[:, 3 * GE:SL], 0).then_inc(pads_set, 1)
            nc.gpsimd.memset(dst_nat[:, 3 * GE:SL], -1).then_inc(pads_set, 1)
            nc.gpsimd.memset(nodes[:, NB - 1, :], 0.0).then_inc(node_pad_set, 1)
            nc.gpsimd.memset(ident[:, :], 0.0).then_inc(node_pad_set, 1)
            nc.gpsimd.memset(before[:, :], 1.0).then_inc(node_pad_set, 1)
            nc.gpsimd.memset(ones[:, :], 1.0).then_inc(consts, 1)
            nc.gpsimd.memset(eps[:, :], EPS).then_inc(consts, 1)
            nc.gpsimd.iota(iota1[:, :], [[1, P]], base=1, channel_multiplier=0,
                           allow_small_or_imprecise_dtypes=True).then_inc(consts, 1)
            nc.gpsimd.iota(part[:, :], [[0, 1]], base=0, channel_multiplier=1,
                           allow_small_or_imprecise_dtypes=True).then_inc(consts, 1)
            nc.gpsimd.iota(block_first[:, :], [[P, NB]], base=0, channel_multiplier=0,
                           allow_small_or_imprecise_dtypes=True).then_inc(consts, 1)
            pool.wait_ge(node_pad_set, 3)
            nc.gpsimd.affine_select(out=ident[:, :], in_=ident[:, :], compare_op=ALU.not_equal, fill=1.0,
                                    base=0, pattern=[[-1, P]], channel_multiplier=1).then_inc(consts, 1)
            nc.gpsimd.affine_select(out=before[:, :], in_=before[:, :], compare_op=ALU.is_gt, fill=0.0,
                                    base=0, pattern=[[1, P]], channel_multiplier=-1).then_inc(consts, 1)
            pool.dma_start(nodes[0:LAST, NB - 1, :], x[(NB - 1) * P:N, :]).then_inc(x_last_in, 16)
            x_blocks = x[0:(NB - 1) * P, :].rearrange("(b p) d -> b p d", p=P)
            for u in range(2):
                pool.dma_start(nodes[:, u, :], x_blocks[u]).then_inc(x_in[u], 16)
            with pool.Fori(1, NB // 2) as i:
                for u in range(2):
                    pool.wait_ge(x_in[u], 16 * i)
                    pool.dma_start(nodes[:, 2 * i + u, :], x_blocks[2 * i + u]).then_inc(x_in[u], 16)
            for u in range(2):
                pool.wait_ge(stored[u], 16 * (NB // 2))
            pool.wait_ge(last_stored, 16)
            last_row = pool.to_reg(NB * P * R - 1)

            def gather_round(i):
                for u in range(SLOTS):
                    pool.wait_ge(rows_ready[u], i + 1)
                    if not isinstance(i, int):
                        pool.wait_ge(group_summed[u], i)
                    pool.sem_inc(pool_carrier, 1)
                    for j in range(J):
                        pool.indirect_dma_start(messages[:, u, j * D:(j + 1) * D], None, table,
                                                bass.IndirectOffsetOnAxis(ap=row_slots[:, u, j:j + 1], axis=0),
                                                bounds_check=last_row).then_inc(gathered[u], 16)

            gather_round(0)
            with pool.Fori(1, ROUNDS) as i:
                gather_round(i)
            pool.wait_ge(tables_ready, 1)
            wide_flag = pool.value_load(flag_i[0:1, 0:1], min_val=0, max_val=1)
            with pool.If(wide_flag > 0):
                with pool.Fori(0, NG) as g:
                    pool.wait_ge(wide_rows, g + 1)
                    pool.sem_inc(pool_carrier, 1)
                    for j in range(J):
                        pool.indirect_dma_start(messages[:, 0, j * D:(j + 1) * D], None, table,
                                                bass.IndirectOffsetOnAxis(ap=row_slots[:, 0, j:j + 1], axis=0),
                                                bounds_check=last_row).then_inc(wide_gathered, 16)

        @block.scalar
        def _(act):
            for s in (ffn_norm_t, ffn_gelu):
                act.sem_inc(s, 1)
            for t in range(GT):
                act.wait_ge(turned, t + 1)
                nc.scalar.activation(gather_rows[:, t * P:(t + 1) * P, :].rearrange("p g j -> p j g"),
                                     banks[t][:, :].rearrange("p (j g) -> p j g", j=J), ACT.Copy).then_inc(turned_by_act, 1)

            def deviate(b, u):
                act.wait_ge(norm_step, 3 * b + 2)
                nc.scalar.activation(deviation[:, u, :], moments[:, u, 1:2], ACT.Sqrt, bias=eps[:, 0:1]).then_inc(norm_deviation, 1)

            def turn(b, u):
                act.wait_ge(norm_turned, b + 1)
                if not isinstance(b, int) or b > 1:
                    act.wait_ge(product_ready, 5 * (b - 1))
                nc.scalar.activation(normed_t[:, u, :, :].rearrange("p k n -> p (k n)"), banks[5 + u][:, 0:D],
                                     ACT.Copy).then_inc(norm_t_ready, 1)

            def evacuate(b, u, turn_no):
                if not isinstance(turn_no, int) or turn_no > 0:
                    act.wait_ge(stored[u], 16 * turn_no)
                for k in range(2):
                    act.wait_ge(product_ready, 5 * b + k + 1)
                    nc.scalar.activation(stage[:, u, k * BANK:(k + 1) * BANK], banks[k][:, :], ACT.Copy)\
                        .then_inc(bank_free[k], 1)

            def block_pair(i):
                for u in range(2):
                    b = 2 * i + u
                    deviate(b + 1, 1 - u)
                    turn(b + 1, 1 - u)
                    evacuate(b, u, i)

            act.wait_ge(consts, CONSTS)
            deviate(0, 0)
            turn(0, 0)
            block_pair(0)
            with act.Fori(1, NB // 2) as i:
                block_pair(i)
            evacuate(NB - 1, 0, NB // 2)

            def fill(g, u):
                nc.scalar.activation(row_slots[:, u, :], gather_rows[:, g, :], ACT.Copy).then_inc(rows_ready[u], 1)

            def refill(i, slots):
                for u in slots:
                    act.wait_ge(gathered[u], 64 * (i + 1))
                    fill(SLOTS * (i + 1) + u, u)

            def ffn_deviate_and_turn(b):
                act.wait_ge(ffn_step, 8 * b + 4)
                nc.scalar.activation(deviation[:, 0, :], moments[:, 0, 1:2], ACT.Sqrt, bias=eps[:, 0:1]).then_inc(ffn_deviation, 1)
                act.wait_ge(ffn_turned, b + 2)
                act.wait_ge(ffn_up, b + 1)
                nc.scalar.activation(normed_t[:, 0, :, :].rearrange("p k n -> p (k n)"), banks[4][:, 0:D],
                                     ACT.Copy).then_inc(ffn_norm_t, 1)

            def ffn_activate(b):
                act.wait_ge(ffn_up, b + 2)
                act.wait_ge(ffn_down, b + 1)
                for m in range(HC):
                    last = nc.scalar.activation(hidden[:, m, :], banks[5 + m // 4][:, m % 4 * P:(m % 4 + 1) * P],
                                                ACT.Gelu_apprx_tanh, bias=b1_col[:, m:m + 1])
                last.then_inc(ffn_gelu, 1)

            act.wait_ge(turned_by_act, GT)
            act.wait_ge(small_in, 16 * 5)
            act.wait_ge(tables_ready, 1)
            for u in range(SLOTS):
                fill(u, u)
            with act.Fori(0, ROUNDS) as i:
                b = act.value_load(round_block[0:1, bass.ds(i, 1)], min_val=0, max_val=NB - 1)
                busy = act.value_load(round_busy[0:1, bass.ds(i, 1)], min_val=0, max_val=1)
                with act.If(busy > 0):
                    ffn_deviate_and_turn(b)
                refill(i, (0, 1))
                with act.If(busy > 0):
                    ffn_activate(b)
                refill(i, (2, 3))
            wide_flag = act.value_load(flag_i[0:1, 0:1], min_val=0, max_val=1)
            with act.If(wide_flag > 0):
                with act.Fori(0, NG) as g:
                    act.wait_ge(wide_group_done, g + 1)
                    nc.scalar.activation(row_slots[:, 0, :], gather_rows[:, g, :], ACT.Copy).then_inc(wide_rows, 1)
            with act.Fori(0, NB) as b:
                left = act.value_load(left_over[0:1, bass.ds(b, 1)], min_val=0, max_val=1)
                with act.If(left > 0):
                    ffn_deviate_and_turn(b)
                    ffn_activate(b)

        @block.tensor
        def _(pe):
            for s in (ffn_turned, ffn_up, ffn_down):
                pe.sem_inc(s, 1)
            pe.wait_ge(consts, CONSTS)
            for k, (table_nat, made) in enumerate(((row_nat, 1), (key_nat, 2), (dst_f, 3))):
                if k == 0:
                    pe.wait_ge(rows_made, 1)
                else:
                    pe.wait_ge(keys_made, k)
                for t in range(GT):
                    n = k * GT + t
                    if k == 1:
                        pe.wait_ge(turned_by_act, t + 1)
                    if k == 2:
                        pe.wait_ge(turned_by_dve, t + 1)
                    for j in range(J):
                        last = nc.tensor.transpose(banks[t][:, j * P:(j + 1) * P],
                                                   table_nat[:, t * GE + j * P:t * GE + (j + 1) * P], ident[:, :])
                    last.then_inc(turned, 1)
            for t in range(GT):
                last = nc.tensor.matmul(banks[4][:, t * P:(t + 1) * P], gmin[:, t:t + 1].broadcast_to([P, P]),
                                        ident[:, :], start=True, stop=True)
            nc.tensor.matmul(banks[5][:, 0:GT], ones[:, :], wide[:, :], start=True, stop=True).then_inc(spread, 1)

            def turn(b, u):
                pe.wait_ge(norm_ready, b + 1)
                for k in range(KC):
                    last = nc.tensor.transpose(banks[5 + u][:, k * P:(k + 1) * P], normed[:, u, k * P:(k + 1) * P], ident[:, :])
                last.then_inc(norm_turned, 1)

            def products(b, u):
                pe.wait_ge(norm_t_ready, b + 1)
                for n in range(5):
                    width = BANK if n < 4 else D
                    if not isinstance(b, int) or b > 0:
                        pe.wait_ge(bank_free[n], b)
                    for k in range(KC):
                        last = nc.tensor.matmul(banks[n][:, 0:width], normed_t[:, u, k, :],
                                                rel_sb[:, k, n * BANK:n * BANK + width], start=(k == 0), stop=(k == KC - 1))
                    last.then_inc(product_ready, 1)

            pe.wait_ge(turned_by_dve, 2 * GT + 1)
            turn(0, 0)
            pe.wait_ge(rel_in, 16 * 2 * KC)
            def block_pair(i):
                for u in range(2):
                    b = 2 * i + u
                    turn(b + 1, 1 - u)
                    products(b, u)

            block_pair(0)
            with pe.Fori(1, NB // 2) as i:
                block_pair(i)
            products(NB - 1, 0)

            for n in range(5):
                pe.wait_ge(bank_free[n], NB)
            def sum_group(i, u):
                pe.wait_ge(onehot_ready[u], i + 1)
                pe.wait_ge(gathered[u], 64 * (i + 1))
                if not isinstance(i, int):
                    pe.wait_ge(sum_taken[u], 2 * i)
                for j in range(J):
                    last = nc.tensor.matmul(banks[u][:, 0:D], onehot[:, u, j, :], messages[:, u, j * D:(j + 1) * D],
                                            start=(j == 0), stop=(j == J - 1))
                last.then_inc(group_summed[u], 1)

            def ffn_turn(b):
                pe.wait_ge(ffn_norm, b + 1)
                pe.wait_ge(ffn_norm_t, b + 1)
                for k in range(KC):
                    last = nc.tensor.transpose(banks[4][:, k * P:(k + 1) * P], normed[:, 0, k * P:(k + 1) * P], ident[:, :])
                last.then_inc(ffn_turned, 1)

            def ffn_first(b):
                pe.wait_ge(ffn_norm_t, b + 2)
                pe.wait_ge(ffn_gelu, b + 1)
                for m in range(HC):
                    for k in range(KC):
                        last = nc.tensor.matmul(banks[5 + m // 4][:, m % 4 * P:(m % 4 + 1) * P],
                                                w1_sb[:, k, m * P:(m + 1) * P], normed_t[:, 0, k, :],
                                                start=(k == 0), stop=(k == KC - 1))
                last.then_inc(ffn_up, 1)

            def ffn_second(b):
                pe.wait_ge(ffn_gelu, b + 2)
                for m in range(HC):
                    last = nc.tensor.matmul(banks[7][:, 0:D], hidden[:, m, :], w2_sb[:, m, :],
                                            start=(m == 0), stop=(m == HC - 1))
                last.then_inc(ffn_down, 1)

            pe.wait_ge(ffn_w_in, 32)
            pe.wait_ge(tables_ready, 1)
            for u in range(SLOTS):
                sum_group(0, u)
            with pe.Fori(1, ROUNDS) as i:
                b = pe.value_load(round_block[0:1, bass.ds(i, 1)], min_val=0, max_val=NB - 1)
                busy = pe.value_load(round_busy[0:1, bass.ds(i, 1)], min_val=0, max_val=1)
                sum_group(i, 0)
                sum_group(i, 1)
                with pe.If(busy > 0):
                    ffn_turn(b)
                sum_group(i, 2)
                with pe.If(busy > 0):
                    ffn_first(b)
                sum_group(i, 3)
                with pe.If(busy > 0):
                    ffn_second(b)

            wide_flag = pe.value_load(flag_i[0:1, 0:1], min_val=0, max_val=1)
            with pe.If(wide_flag > 0):
                pe.wait_ge(group_summed[0], ROUNDS)
                pe.sem_inc(wide_group_done, 1)
                with pe.Fori(0, NG) as g:
                    with pe.Fori(0, NB) as b:
                        pe.wait_ge(wide_gathered, 64 * (g + 1))
                        pe.wait_ge(wide_onehot, g * NB + b + 1)
                        for j in range(J):
                            last = nc.tensor.matmul(banks[0][:, 0:D], onehot[:, 0, j, :], messages[:, 0, j * D:(j + 1) * D],
                                                    start=(j == 0), stop=(j == J - 1))
                        last.then_inc(wide_summed, 1)
                    pe.wait_ge(wide_added, NB * (g + 1))
                    pe.sem_inc(wide_group_done, 1)

            with pe.Fori(0, NB) as b:
                left = pe.value_load(left_over[0:1, bass.ds(b, 1)], min_val=0, max_val=1)
                with pe.If(left > 0):
                    ffn_turn(b)
                    ffn_first(b)
                    ffn_second(b)

            for r in range(8):
                pe.wait_ge(counts_in, r + 1)
                nc.tensor.matmul(banks[0][:, 0:15], ones[:, :], pick_counts[:, :], start=True, stop=True).then_inc(counts_out, 1)
            pe.wait_ge(counts_in, 9)
            nc.tensor.matmul(banks[0][:, 0:1], ones[:, :], above_count[:, :], start=True, stop=True)
            nc.tensor.matmul(banks[1][:, 0:NB], ones[:, :], tied[:, :], start=True, stop=True)
            nc.tensor.matmul(banks[2][:, 0:NB], before[:, :], tied[:, :], start=True, stop=True).then_inc(counts_out, 1)

        @block.vector
        def _(dve):
            V = nc.vector
            count = {}

            def link(s, ins):
                count[s.name] = count.get(s.name, 0) + 1
                ins.then_inc(s, 1)
                dve.wait_ge(s, count[s.name])

            for k in range(3):
                dve.wait_ge(edges_in[k], 48)
            V.scalar_tensor_tensor(row_nat, src_nat, float(R), type_nat, ALU.mult, ALU.add).then_inc(rows_made, 1)
            link(index_step, V.tensor_copy(dst_f, dst_nat))
            link(index_step, V.tensor_scalar(key_nat, dst_f, 0.0, 16384.0, ALU.is_lt, ALU.mult))
            link(index_step, V.tensor_tensor(key_nat, key_nat, dst_f, ALU.add))
            link(index_step, V.tensor_reduce(gmin[:, :], key_nat.rearrange("p (t e) -> p t e", e=GE), AX.X, ALU.min))
            link(index_step, V.tensor_reduce(gmax[:, :], dst_f.rearrange("p (t e) -> p t e", e=GE), AX.X, ALU.max))
            link(index_step, V.tensor_scalar_min(gmin[:, :], gmin[:, :], float(N - 1)))
            link(index_step, V.tensor_tensor(fits[:, :], gmax[:, :], gmin[:, :], ALU.subtract))
            link(index_step, V.tensor_scalar(wide[:, :], fits[:, :], float(P), None, ALU.is_ge))
            link(index_step, V.tensor_scalar(fits[:, :], wide[:, :], -1.0, 1.0, ALU.mult, ALU.add))
            dve.wait_ge(rows_made, 1)
            link(index_step, V.tensor_scalar(masked_i, dst_nat, P - 1, None, ALU.bitwise_and))
            link(index_step, V.tensor_scalar(key_nat, masked_i, 1.0, None, ALU.add))
            for t in range(GT):
                part_of = slice(t * GE, (t + 1) * GE)
                link(index_step, V.tensor_scalar(valid_f[:, part_of], dst_f[:, part_of], 0.0, fits[:, t:t + 1], ALU.is_ge, ALU.mult))
            V.tensor_tensor(key_nat, key_nat, valid_f, ALU.mult).then_inc(keys_made, 1)
            for t in range(GT):
                part_of = slice(t * GE, (t + 1) * GE)
                last = V.tensor_scalar(dst_f[:, part_of], dst_f[:, part_of], 1.0, wide[:, t:t + 1], ALU.add, ALU.mult)
            last.then_inc(keys_made, 1)
            for k, to in enumerate((window_keys, wide_keys)):
                for t in range(GT):
                    dve.wait_ge(turned, (k + 1) * GT + t + 1)
                    V.tensor_copy(to[:, t * P:(t + 1) * P, :].rearrange("p g j -> p j g"),
                                  banks[t][:, :].rearrange("p (j g) -> p j g", j=J)).then_inc(turned_by_dve, 1)
            dve.wait_ge(spread, 1)
            link(index_step, V.tensor_copy(gmin_i[:, :], banks[4][:, :]))
            link(index_step, V.tensor_reduce(any_wide[:, :], banks[5][:, 0:GT], AX.X, ALU.max))
            link(index_step, V.tensor_scalar_min(any_wide[:, :], any_wide[:, :], 1.0))
            V.tensor_copy(flag_i[:, :], any_wide[0:1, :]).then_inc(turned_by_dve, 1)
            link(index_step, V.tensor_scalar(gtmp_i[:, :], gmin_i[:, :], P - 1, None, ALU.bitwise_and))
            link(index_step, V.tensor_scalar(low_mask[:, :], gtmp_i[:, :], part[:, 0:1], None, ALU.is_le))
            link(index_step, V.tensor_scalar(high_mask[:, :], low_mask[:, :], -1.0, 1.0, ALU.mult, ALU.add))
            link(index_step, V.tensor_scalar(first_block[:, :], gmin_i[:, :], 7, None, ALU.logical_shift_right))
            V.memset(zeros[:, :], 0.0)
            V.memset(acc[:, NB, :], 0.0)
            link(index_step, V.memset(ready[:, :, :], float(NB - 1)))
            link(index_step, V.tensor_copy(first_block_f[:, :], first_block[0:1, :]))
            link(index_step, V.tensor_reduce(ready[:, 0, 0:P], first_block_f[:, :].rearrange("p (i u) -> p i u", u=SLOTS), AX.X, ALU.min))
            for n in range(7):
                link(index_step, V.tensor_tensor(ready[:, (n + 1) % 2, 0:P], ready[:, n % 2, 0:P],
                                                 ready[:, n % 2, 1 << n:(1 << n) + P], ALU.min))
            link(index_step, V.tensor_scalar(any_wide[:, :], any_wide[:, :], -1.0, 1.0, ALU.mult, ALU.add))
            link(index_step, V.tensor_scalar(ready[:, 1, 0:P], ready[:, 1, 0:P], any_wide[0:1, 0:1], None, ALU.mult))
            link(index_step, V.memset(one_row[:, :], 1.0))
            link(index_step, V.memset(round_block[:, 0:1], 0))
            link(index_step, V.tensor_tensor_scan(done_f[:, :], one_row[:, :], ready[:, 1, 0:P], 0.0, ALU.add, ALU.min))
            link(index_step, V.tensor_copy(round_block[:, 1:P + 1], done_f[:, :]))
            link(index_step, V.tensor_tensor(round_busy[:, :], round_block[:, 1:P + 1], round_block[:, 0:P], ALU.subtract))
            link(index_step, V.tensor_scalar(block_no[:, :], block_first[0:1, :], 1.0 / P, None, ALU.mult))
            link(index_step, V.tensor_scalar(left_over[:, :], block_no[:, :], done_f[0:1, ROUNDS - 1:ROUNDS], None, ALU.is_ge))
            dve.wait_ge(turned_by_dve, 2 * GT + 1)
            dve.sem_inc(tables_ready, 1)

            NORM_STEPS = 3

            def norm(b, u):
                V.bn_stats(stats[:, u, :], nodes[:, b, :]).then_inc(norm_step, 1)
                dve.wait_ge(norm_step, NORM_STEPS * b + 1)
                dve.sem_inc(wait_carrier, 1)
                V.bn_aggr(moments[:, u, :], stats[:, u, :]).then_inc(norm_step, 1)
                dve.wait_ge(norm_deviation, b + 1)
                V.reciprocal(rstd[:, u, :], deviation[:, u, :]).then_inc(norm_step, 1)
                dve.wait_ge(norm_step, NORM_STEPS * b + 3)
                if not isinstance(b, int) or b > 1:
                    dve.wait_ge(norm_turned, b - 1)
                V.tensor_scalar(normed[:, u, :], nodes[:, b, :], moments[:, u, 0:1], rstd[:, u, 0:1],
                                ALU.subtract, ALU.mult).then_inc(norm_ready, 1)

            def evacuate(b, u):
                for k in (2, 3):
                    dve.wait_ge(product_ready, 5 * b + k + 1)
                    V.tensor_copy(stage[:, u, k * BANK:(k + 1) * BANK], banks[k][:, :])\
                        .then_inc(bank_free[k], 1)
                dve.wait_ge(product_ready, 5 * b + 5)
                V.tensor_copy(acc[:, b, :], banks[4][:, 0:D]).then_inc(bank_free[4], 1)

            dve.wait_ge(x_in[0], 16)
            norm(0, 0)
            def block_pair(i, last_pair=False):
                dve.wait_ge(x_in[1], 16 * (i + 1))
                norm(2 * i + 1, 1)
                if not isinstance(i, int) or i > 0:
                    dve.wait_ge(stored[0], 16 * i)
                evacuate(2 * i, 0)
                if last_pair:
                    dve.wait_ge(x_last_in, 16)
                else:
                    dve.wait_ge(x_in[0], 16 * (i + 2))
                norm(2 * i + 2, 0)
                if not isinstance(i, int) or i > 0:
                    dve.wait_ge(stored[1], 16 * i)
                evacuate(2 * i + 1, 1)

            block_pair(0)
            with dve.Fori(1, NB // 2 - 1) as i:
                block_pair(i)
            block_pair(NB // 2 - 1, last_pair=True)
            dve.wait_ge(stored[0], 16 * (NB // 2))
            evacuate(NB - 1, 0)

            def build(g, u, turn_no):
                if not isinstance(turn_no, int) or turn_no > 0:
                    dve.wait_ge(group_summed[u], turn_no)
                for j in range(J):
                    last = V.tensor_scalar(onehot[:, u, j, :], iota1[:, :], window_keys[:, g, j:j + 1], None, ALU.is_equal)
                last.then_inc(onehot_ready[u], 1)

            dve.wait_ge(turned_by_dve, 2 * GT + 1)
            dve.wait_ge(bank_free[4], NB)
            build(0, 0, 0)
            build(1, 1, 0)

            def add_group(i, u):
                g = SLOTS * i + u
                build(g + 2, (u + 2) % SLOTS, i + (u + 2) // SLOTS)
                at = slice(g, g + 1) if isinstance(g, int) else bass.ds(g, 1)
                b0 = dve.value_load(first_block[0:1, at], min_val=0, max_val=NB - 1)
                dve.wait_ge(group_summed[u], i + 1)
                if u:
                    dve.wait_ge(sum_taken[u - 1], 2 * (i + 1))
                elif not isinstance(i, int):
                    dve.wait_ge(sum_taken[SLOTS - 1], 2 * i)
                for k, mask in enumerate((low_mask, high_mask)):
                    V.scalar_tensor_tensor(acc[:, b0 + k, :], banks[u][:, 0:D], mask[:, at], acc[:, b0 + k, :],
                                           ALU.mult, ALU.add).then_inc(sum_taken[u], 1)

            FS = 8

            def step(b, n, ins):
                ins.then_inc(ffn_step, 1)
                dve.wait_ge(ffn_step, FS * b + n)

            def ffn_enter(b):
                step(b, 1, V.scalar_tensor_tensor(x1[:, :], acc[:, b, :], SCALE, nodes[:, b, :], ALU.mult, ALU.add))
                step(b, 2, V.tensor_tensor(x1[:, :], x1[:, :], bias_b[:, :], ALU.add))
                V.bn_stats(stats[:, 0, :], x1[:, :]).then_inc(ffn_step, 1)
                dve.wait_ge(ffn_step, FS * b + 3)
                dve.sem_inc(wait_carrier, 1)
                step(b, 4, V.bn_aggr(moments[:, 0, :], stats[:, 0, :]))
                dve.wait_ge(ffn_deviation, b + 1)
                step(b, 5, V.reciprocal(rstd[:, 0, :], deviation[:, 0, :]))
                dve.wait_ge(ffn_turned, b + 1)
                V.tensor_scalar(normed[:, 0, :], x1[:, :], moments[:, 0, 0:1], rstd[:, 0, 0:1],
                                ALU.subtract, ALU.mult).then_inc(ffn_norm, 1)
                dve.wait_ge(ffn_norm, b + 1)
                V.tensor_tensor(nodes[:, b, :], x1[:, :], normed[:, 0, :], ALU.add).then_inc(ffn_step, 1)
                V.tensor_tensor_reduce(out=y_biased[:, :], in0=normed[:, 0, :], in1=wr_b[:, :], scale=1.0, scalar=0.0,
                                       op0=ALU.mult, op1=ALU.add, accum_out=w_block[:, 0:1]).then_inc(ffn_step, 1)
                dve.wait_ge(ffn_step, FS * b + 7)
                V.tensor_scalar(w_block[:, 1:2], w_block[:, 0:1], br_b[:, 0:1], None, ALU.add)
                V.tensor_scalar(w_all[:, bass.ds(b, 1)], w_block[:, 0:1], br_b[:, 0:1], None, ALU.add).then_inc(ffn_step, 1)

            def ffn_leave(b):
                dve.wait_ge(ffn_step, FS * b + 8)
                dve.wait_ge(ffn_down, b + 2)
                V.tensor_tensor(y_biased[:, :], banks[7][:, 0:D], b2_b[:, :], ALU.add).then_inc(ffn_done, 1)
                dve.wait_ge(ffn_done, 2 * b + 1)
                V.tensor_scalar(acc[:, b, :], y_biased[:, :], w_block[:, 1:2], None, ALU.mult).then_inc(ffn_done, 1)

            dve.wait_ge(small_in, 16 * 5)
            for u in range(SLOTS):
                add_group(0, u)
            with dve.Fori(1, ROUNDS) as i:
                b = dve.value_load(round_block[0:1, bass.ds(i, 1)], min_val=0, max_val=NB - 1)
                busy = dve.value_load(round_busy[0:1, bass.ds(i, 1)], min_val=0, max_val=1)
                add_group(i, 0)
                with dve.If(busy > 0):
                    ffn_enter(b)
                for u in range(1, SLOTS):
                    add_group(i, u)
                with dve.If(busy > 0):
                    ffn_leave(b)
            dve.wait_ge(sum_taken[SLOTS - 1], 2 * ROUNDS)

            wide_flag = dve.value_load(flag_i[0:1, 0:1], min_val=0, max_val=1)
            with dve.If(wide_flag > 0):
                with dve.Fori(0, NG) as g:
                    with dve.Fori(0, NB) as b:
                        n = g * NB + b
                        V.tensor_scalar(shifted[:, :], wide_keys[:, g, :], block_first[:, bass.ds(b, 1)], None,
                                        ALU.subtract).then_inc(wide_step, 1)
                        dve.wait_ge(wide_step, n + 1)
                        for j in range(J):
                            last = V.tensor_scalar(onehot[:, 0, j, :], iota1[:, :], shifted[:, j:j + 1], None, ALU.is_equal)
                        last.then_inc(wide_onehot, 1)
                        dve.wait_ge(wide_summed, n + 1)
                        V.tensor_tensor(acc[:, b, :], banks[0][:, 0:D], acc[:, b, :], ALU.add).then_inc(wide_added, 1)
                dve.wait_ge(wide_added, NG * NB)

            with dve.Fori(0, NB) as b:
                left = dve.value_load(left_over[0:1, bass.ds(b, 1)], min_val=0, max_val=1)
                with dve.If(left > 0):
                    ffn_enter(b)
                    ffn_leave(b)
            dve.wait_ge(ffn_done, 2 * NB)

            w_bits = w_all[:, :].bitcast(I32)
            link(pick_step, V.tensor_scalar(sign_i[:, :], w_bits, 31, 0x7FFFFFFF, ALU.arith_shift_right, ALU.bitwise_and))
            link(pick_step, V.tensor_tensor(key_i[:, :], w_bits, sign_i[:, :], ALU.bitwise_xor))
            link(pick_step, V.tensor_scalar(half_i[:, :], key_i[:, :], 16, None, ALU.arith_shift_right))
            link(pick_step, V.tensor_copy(key_hi[:, :], half_i[:, :]))
            link(pick_step, V.tensor_scalar(half_i[:, :], key_i[:, :], 0xFFFF, None, ALU.bitwise_and))
            link(pick_step, V.tensor_copy(key_lo[:, :], half_i[:, :]))
            link(pick_step, V.tensor_scalar(real[:, :], part[:, :], float(LAST), None, ALU.is_lt))
            link(pick_step, V.tensor_scalar(pad_key[:, :], real[:, :], 40000.0, -40000.0, ALU.mult, ALU.add))
            link(pick_step, V.tensor_scalar(key_hi[:, NB - 1:NB], key_hi[:, NB - 1:NB], real[:, 0:1], pad_key[:, 0:1], ALU.mult, ALU.add))
            link(pick_step, V.tensor_scalar(digits[:, :], iota1[:, 0:15], 1.0, None, ALU.mult))

            def radix_round(r, keys, shift):
                link(pick_step, V.tensor_scalar(candidates[:, :], digits[:, :], float(1 << shift), floor_[:, 0:1], ALU.mult, ALU.add))
                link(pick_step, V.tensor_tensor(compared[:, :, :], keys.unsqueeze(1).broadcast_to([P, 15, NB]),
                                                candidates[:, :].unsqueeze(2).broadcast_to([P, 15, NB]), ALU.is_ge))
                V.tensor_reduce(pick_counts[:, :], compared[:, :, :], AX.X, ALU.add).then_inc(counts_in, 1)
                dve.wait_ge(counts_out, r + 1)
                link(pick_step, V.tensor_scalar(reached[:, :], banks[0][:, 0:15], float(SELECTED), None, ALU.is_ge))
                link(pick_step, V.tensor_reduce(passed[:, :], reached[:, :], AX.X, ALU.add))
                link(pick_step, V.scalar_tensor_tensor(floor_[:, :], passed[:, :], float(1 << shift), floor_[:, :], ALU.mult, ALU.add))

            link(pick_step, V.memset(floor_[:, :], -32768.0))
            for r in range(4):
                radix_round(r, key_hi[:, :], 12 - 4 * r)
            link(pick_step, V.tensor_scalar(above[:, :], key_hi[:, :], floor_[:, 0:1], 65536.0, ALU.is_gt, ALU.mult))
            link(pick_step, V.tensor_scalar(tied[:, :], key_hi[:, :], floor_[:, 0:1], None, ALU.is_equal))
            link(pick_step, V.tensor_scalar(key_lo[:, :], key_lo[:, :], 1.0, None, ALU.add))
            link(pick_step, V.tensor_tensor(key_lo[:, :], key_lo[:, :], tied[:, :], ALU.mult))
            link(pick_step, V.tensor_tensor(key_lo[:, :], key_lo[:, :], above[:, :], ALU.add))
            link(pick_step, V.tensor_scalar(key_lo[:, :], key_lo[:, :], -1.0, None, ALU.add))
            link(pick_step, V.memset(floor_[:, :], 0.0))
            for r in range(4):
                radix_round(4 + r, key_lo[:, :], 12 - 4 * r)
            link(pick_step, V.tensor_scalar(above[:, :], key_lo[:, :], floor_[:, 0:1], None, ALU.is_gt))
            link(pick_step, V.tensor_scalar(tied[:, :], key_lo[:, :], floor_[:, 0:1], None, ALU.is_equal))
            V.tensor_reduce(above_count[:, :], above[:, :], AX.X, ALU.add).then_inc(counts_in, 1)
            dve.wait_ge(counts_out, 9)
            link(pick_step, V.tensor_scalar(quota[:, :], banks[0][:, 0:1], -1.0, float(SELECTED), ALU.mult, ALU.add))
            link(pick_step, V.memset(tie_base[:, 0:1], 0.0))
            link(pick_step, V.tensor_copy(key_hi[:, :], banks[1][:, 0:NB]))
            link(pick_step, V.tensor_tensor_scan(tie_base[:, 1:NB + 1], key_hi[:, :], zeros[:, :], 0.0, ALU.add, ALU.add))
            link(pick_step, V.tensor_tensor(keep[:, :], banks[2][:, 0:NB], tie_base[:, 0:NB], ALU.add))
            link(pick_step, V.tensor_scalar(keep[:, :], keep[:, :], quota[:, 0:1], None, ALU.is_lt))
            link(pick_step, V.tensor_tensor(keep[:, :], keep[:, :], tied[:, :], ALU.mult))
            link(pick_step, V.tensor_tensor(keep[:, :], keep[:, :], above[:, :], ALU.add))

            with dve.Fori(0, NB) as b:
                V.scalar_tensor_tensor(nodes[:, b, :], acc[:, b, :], keep[:, bass.ds(b, 1)], nodes[:, b, :],
                                       ALU.mult, ALU.add).then_inc(output_ready, 1)


_NAMES = ["x", "src", "dst", "edge_type_8", "L0_gnn_weight", "L0_gnn_h_bias", "L0_gnn_loop_weight",
          "L0_ffn_wr", "L0_ffn_br", "L0_ffn_w1", "L0_ffn_b1", "L0_ffn_w2", "L0_ffn_b2"]


def kernel(**inputs):
    import numpy as _np
    import concourse.bacc as _bacc
    from concourse import mybir as _mybir
    from concourse.bass_utils import run_bass_kernel_spmd as _run

    nc = _bacc.Bacc("TRN2", target_bir_lowering=False, num_devices=1)
    arrays, args = {}, []
    for name in _NAMES:
        a = _np.ascontiguousarray(inputs[name])
        arrays[f"in_{name}"] = a
        args.append(nc.dram_tensor(f"in_{name}", a.shape, _mybir.dt.from_np(a.dtype), kind="ExternalInput").ap())
    shape = _np.shape(inputs["x"])
    args.append(nc.dram_tensor("node_out", shape, _mybir.dt.float32, kind="ExternalOutput").ap())
    gnn_ffn_program(nc, *args)
    r = _run(nc, [arrays], core_ids=[0])
    return r.results[0]["node_out"]
```

```python
import concourse.bass as bass
from concourse import mybir
from contextlib import ExitStack

P = 128
F32 = mybir.dt.float32
BF16 = mybir.dt.bfloat16
I32 = mybir.dt.int32
ALU = mybir.AluOpType
ACT = mybir.ActivationFunctionType
AX = mybir.AxisListType


def gnn_ffn_program(nc, x, src, dst, edge_type, rel_w, h_bias, loop_w, wr, br, w1, b1, w2, b2, out):
    N, D = x.shape
    E = src.shape[0]
    R = rel_w.shape[0]
    H = w1.shape[1]
    KC = D // P
    HC = H // P
    NB = -(-N // P)
    LAST = N - (NB - 1) * P
    CH = 7
    NCH = NB // CH
    J = 4
    GP = 2
    GE = J * P
    SLOTS = 4
    NG_FULL = E // GE
    NG = -(-(-(-E // GE)) // SLOTS) * SLOTS
    NGT = NG + SLOTS
    ROUNDS = NG // SLOTS
    CONSTS = 7
    GT = 4
    W = P // R
    KR = KC * R
    OPEN = P + W
    PIPE = 2
    STEPS = ROUNDS + NB + PIPE + 1
    FIELD = 64
    DRAIN = PIPE + 1
    SELECTED = max(1, int(0.5 * N)) - 1
    SCALE = 0.7071067811865476
    EPS = 1e-5
    FFN_STEPS = 7
    BANK = 512
    assert NB == NCH * CH and NCH % 2 == 1 and NGT <= GT * P and W * R == P and NB < FIELD and ROUNDS % 2 == 1

    ctx = ExitStack()
    with ctx:
        def sb(name, shape, dt=F32):
            return ctx.enter_context(nc.sbuf_tensor(name, shape, dt))

        def sem(name):
            return ctx.enter_context(nc.semaphore(name))

        table = nc.dram_tensor("normed_table", [NB * P, D], F32).ap()
        table_chunks = table.rearrange("(c v p) d -> c p v d", p=P, v=CH)

        acc = sb("acc", [P, NB, D])
        nodes = sb("nodes", [P, NB, D])
        messages = sb("messages", [P, SLOTS, J * D])
        rel_sb = sb("rel_sb", [P, KC, R * D])
        w1_sb = sb("w1_sb", [P, KC, H])
        w2_sb = sb("w2_sb", [P, HC, D])
        gather_rows = sb("gather_rows", [P, NGT, J], I32)
        keys = sb("keys", [P, NGT, J], BF16)
        sums = sb("sums", [P, KR, 2 * OPEN])
        closed = sb("closed", [P, KR, P])
        onehot = sb("onehot", [P, SLOTS, J, P])
        hidden = sb("hidden", [P, HC, P])
        flat = acc[:, :, :].rearrange("p b d -> p (b d)")
        def edge_area(k):
            return flat[:, k * GT * GE:(k + 1) * GT * GE]
        src_s, type_s, dst_s = (edge_area(k).bitcast(I32).rearrange("p (t e) -> p t e", t=GT) for k in range(3))
        src_f, key_s = (edge_area(k).rearrange("p (t e) -> p t e", t=GT) for k in (3, 4))
        def row_area(k, dt=F32):
            a = flat[0:1, k * GP * BANK:(k + 1) * GP * BANK]
            return (a if dt is F32 else a.bitcast(dt)).rearrange("p (h g) -> p h g", h=GP)
        gmin_i, block_i = row_area(0, I32), row_area(1, I32)
        offset_i, parity_i = row_area(2, I32), row_area(3, I32)
        block_f, lowest, highest = row_area(4), row_area(5), row_area(10)
        goal, steps_one, steps_goal, highest_goal, entered = (
            flat[0:1, 11 * GP * BANK + k * BANK // 2:11 * GP * BANK + k * BANK // 2 + n]
            for k, n in enumerate((STEPS, STEPS, STEPS, STEPS, STEPS + 3)))
        stage = messages[:, :, :].rearrange("p s (v d) -> p (s v) d", d=D)

        loop_sb = sb("loop_sb", [P, KC, D])
        normed_x = sb("normed_x", [P, D])
        normed_x_t = sb("normed_x_t", [P, KC, P])
        row_slots = sb("row_slots", [P, 2, SLOTS * J], I32)
        position = sb("position", [1, NG], I32)
        round_code = sb("round_code", [1, STEPS], I32)
        many_left_i = sb("many_left_i", [1, 1], I32)
        flag_i = sb("flag_i", [1, 1], I32)
        regular = sb("regular", [P, 1])
        bad = sb("bad", [P, 1])
        violations = sb("violations", [1, 1])
        normed = sb("normed", [P, D])
        normed_t = sb("normed_t", [P, KC, P])
        x1 = sb("x1", [P, D])
        stats = sb("stats", [P, 6])
        moments = sb("moments", [P, 2])
        deviation = sb("deviation", [P, 1])
        rstd = sb("rstd", [P, 1])
        eps = sb("eps", [P, 1])
        zero = sb("zero", [P, 1])
        one = sb("one", [P, 1])
        ident = sb("ident", [P, P])
        iota0 = sb("iota0", [P, P])
        part = sb("part", [P, 1])
        bias_b = sb("bias_b", [P, D])
        b2_b = sb("b2_b", [P, D])
        wr_b = sb("wr_b", [P, D])
        br_b = sb("br_b", [P, 1])
        b1_col = sb("b1_col", [P, HC])
        w_block = sb("w_block", [P, 1])
        w_all = sb("w_all", [P, NB])
        one_rows = one[:, 0:1].broadcast_to([P, P])

        def areas(of):
            at = [0]
            def take(n, dt=F32):
                a = of[:, at[0]:at[0] + n]
                at[0] += n
                return a if dt is F32 else a.bitcast(dt)
            return take

        general_rows_sb, general_messages = (closed[:, h * KR // 2:(h + 1) * KR // 2, :].rearrange("p k n -> p (k n)")
                                             for h in range(2))
        early = areas(hidden[:, :, :].rearrange("p m n -> p (m n)"))
        edge_src, edge_type_i, edge_dst = (early(J, I32) for _ in range(3))
        edge_type_f, edge_dst_f, shifted = (early(J) for _ in range(3))
        of_relation = early(R)
        block_first = early(NB)
        chunk_stats = early(CH * 6).rearrange("p (v s) -> p v s", v=CH)
        chunk_moments = early(2 * CH * 2).rearrange("p (u v s) -> p u v s", u=2, v=CH)
        chunk_deviation, chunk_rstd, chunk_shift = (early(2 * CH).rearrange("p (u v) -> p u v", u=2) for _ in range(3))
        gmin, gspan = (early(GT * GP).rearrange("p (t h) -> p t h", h=GP) for _ in range(2))

        rt = areas(messages[:, :, :].rearrange("p s d -> p (s d)"))
        compared = rt(15 * NB).rearrange("p (d b) -> p d b", d=15)
        before = rt(P)
        pick_counts, digits, candidates, reached = (rt(15) for _ in range(4))
        above_count, floor_, passed, quota, real, pad_key = (rt(1) for _ in range(6))
        tied, above, key_hi, key_lo, zeros, keep = (rt(NB) for _ in range(6))
        key_i, sign_i, half_i = (rt(NB, I32) for _ in range(3))
        tie_base = rt(NB + 1)

        banks = [ctx.enter_context(nc.psum_tensor(f"bank{i}", [P, BANK], F32)) for i in range(8)]

        pads_set = sem("pads_set")
        node_pad_set = sem("node_pad_set")
        consts = sem("consts")
        edges_in = sem("edges_in")
        x_in = [sem(f"x_in{i}") for i in range(2)]
        x_last_in = sem("x_last_in")
        loop_in = sem("loop_in")
        rel_in = sem("rel_in")
        small_in = sem("small_in")
        ffn_w_in = sem("ffn_w_in")
        norm_step = sem("norm_step")
        norm_deviation = sem("norm_deviation")
        norm_scaled = sem("norm_scaled")
        norm_ready = sem("norm_ready")
        stored = [sem(f"stored{i}") for i in range(2)]
        normed_x_in = sem("normed_x_in")
        loop_turned = sem("loop_turned")
        loop_t_ready = sem("loop_t_ready")
        src_f_ready = sem("src_f_ready")
        index_step = sem("index_step")
        keys_flat = sem("keys_flat")
        slab_turned = sem("slab_turned")
        slab_taken = sem("slab_taken")
        spread = sem("spread")
        bad_ready = sem("bad_ready")
        bad_total = sem("bad_total")
        row_step = sem("row_step")
        tables_ready = sem("tables_ready")
        sums_clear = sem("sums_clear")
        rows_ready = sem("rows_ready")
        gathered = [sem(f"gathered{i}") for i in range(SLOTS)]
        onehot_ready = [sem(f"onehot_ready{i}") for i in range(SLOTS // 2)]
        pair_summed = [sem(f"pair_summed{i}") for i in range(SLOTS)]
        sum_taken = [sem(f"sum_taken{i}") for i in range(SLOTS)]
        carried = sem("carried")
        closed_ready = sem("closed_ready")
        slot_cleared = sem("slot_cleared")
        agg_ready = sem("agg_ready")
        agg_taken = sem("agg_taken")
        wait_carrier = sem("wait_carrier")
        pool_carrier = sem("pool_carrier")
        ffn_step = sem("ffn_step")
        ffn_deviation = sem("ffn_deviation")
        ffn_norm = sem("ffn_norm")
        ffn_turned = sem("ffn_turned")
        ffn_norm_t = sem("ffn_norm_t")
        ffn_up = sem("ffn_up")
        ffn_gelu = sem("ffn_gelu")
        ffn_down = sem("ffn_down")
        ffn_done = sem("ffn_done")
        general_in = sem("general_in")
        general_pads = sem("general_pads")
        general_rows = sem("general_rows")
        general_cast = sem("general_cast")
        general_turned = sem("general_turned")
        general_t = sem("general_t")
        general_products = sem("general_products")
        general_message = sem("general_message")
        general_shift = sem("general_shift")
        general_onehot = sem("general_onehot")
        general_summed = sem("general_summed")
        general_added = sem("general_added")
        pick_step = sem("pick_step")
        counts_in = sem("counts_in")
        counts_out = sem("counts_out")
        output_ready = sem("output_ready")
        written = sem("written")

        def phases(eng, i):
            at = slice(i, i + 1) if isinstance(i, int) else bass.ds(i, 1)
            code = eng.value_load(round_code[0:1, at], min_val=0, max_val=8 * FIELD - 1)
            bits = [(code >> (FIELD.bit_length() - 1 + n)) & 1 for n in range(3)]
            leaving = code & (FIELD - 1)
            following = leaving + bits[2]
            entering = following + bits[1]
            return bits, [b.with_bounds(min_val=0, max_val=NB - 1) for b in (entering, following, leaving)], entering + bits[0]

        block = ctx.enter_context(nc.Block())

        @block.sync
        def _(sp):
            full_tiles = NG_FULL // P
            rest = NG_FULL - full_tiles * P
            sp.wait_ge(pads_set, 3)
            for a, to in ((dst, dst_s), (src, src_s), (edge_type, type_s)):
                sp.dma_start(to[:, 0:full_tiles, :], a[0:full_tiles * P * GE].rearrange("(t p e) -> p t e", p=P, e=GE)).then_inc(edges_in, 16)
                sp.dma_start(to[0:rest, full_tiles, :], a[full_tiles * P * GE:NG_FULL * GE].rearrange("(p e) -> p e", e=GE)).then_inc(edges_in, 16)
                sp.dma_start(to[rest:rest + 1, full_tiles, 0:E - NG_FULL * GE],
                             a[NG_FULL * GE:E].rearrange("(p e) -> p e", p=1)).then_inc(edges_in, 16)
            sp.dma_start(loop_sb[:, :, :], loop_w.rearrange("(k p) o -> p k o", p=P)).then_inc(loop_in, 16)

            def store(c, u):
                sp.wait_ge(norm_ready, c + 1)
                sp.dma_start(table_chunks[c], stage[:, u * CH:(u + 1) * CH, :]).then_inc(stored[u], 16)

            store(0, 0)
            store(1, 1)
            sp.wait_ge(x_last_in, 32)
            for k in range(KC):
                sp.dma_start(rel_sb[:, k, :].rearrange("p (r o) -> p r o", r=R),
                             rel_w[:, k * P:(k + 1) * P, :].rearrange("r p o -> p r o")).then_inc(rel_in, 16)
            with sp.Fori(1, NCH // 2) as i:
                for u in range(2):
                    store(2 * i + u, u)
            sp.dma_start(w1_sb[:, :, :], w1.rearrange("(k p) h -> p k h", p=P)).then_inc(ffn_w_in, 16)
            store(NCH - 1, 0)
            for to, a in ((bias_b, h_bias), (b2_b, b2)):
                sp.dma_start(to[:, :], a.rearrange("(o d) -> o d", o=1).broadcast_to([P, D])).then_inc(small_in, 16)
            sp.dma_start(wr_b[:, :], wr.rearrange("d o -> o d").broadcast_to([P, D])).then_inc(small_in, 16)
            sp.dma_start(br_b[:, :], br.rearrange("(o d) -> o d", o=1).broadcast_to([P, 1])).then_inc(small_in, 16)
            sp.dma_start(b1_col[:, :], b1.rearrange("(m p) -> p m", p=P),
                         allow_slow_non_contiguous=True).then_inc(small_in, 16)
            sp.dma_start(w2_sb[:, :, :], w2.rearrange("(m p) d -> p m d", p=P)).then_inc(ffn_w_in, 16)
            for u in range(2):
                sp.wait_ge(stored[u], 16 * (NCH // 2 + 1 - u))
            sp.dma_start(normed_x[:, :], table[0:P, :]).then_inc(normed_x_in, 16)
            with sp.Fori(1, NB) as b:
                sp.wait_ge(loop_turned, b)
                sp.dma_start(normed_x[:, :], table.rearrange("(b p) d -> b p d", p=P)[b]).then_inc(normed_x_in, 16)
            with sp.Fori(0, NB // 4) as q:
                sp.wait_ge(output_ready, 4 * q + 4)
                sp.dma_start(out[0:(NB - 1) * P, :].rearrange("(q b p) d -> q p b d", p=P, b=4)[q],
                             nodes[:, bass.ds(4 * q, 4), :]).then_inc(written, 16)
            sp.wait_ge(output_ready, NB)
            sp.dma_start(out[(NB - 1) * P:N, :], nodes[0:LAST, NB - 1, :]).then_inc(written, 16)
            sp.wait_ge(written, 16 * (NB // 4 + 1))

        @block.gpsimd
        def _(pool):
            nc.gpsimd.memset(dst_s[:, GT - 1, :], -1).then_inc(pads_set, 1)
            nc.gpsimd.memset(src_s[:, GT - 1, :], 0).then_inc(pads_set, 1)
            nc.gpsimd.memset(type_s[:, GT - 1, :], 0).then_inc(pads_set, 1)
            x_chunks = x[0:(NCH - 1) * CH * P, :].rearrange("(c v p) d -> c p v d", p=P, v=CH)
            for c in range(2):
                pool.dma_start(nodes[:, c * CH:(c + 1) * CH, :], x_chunks[c]).then_inc(x_in[c], 16)
            nc.gpsimd.memset(nodes[:, NB - 1, :], 0.0).then_inc(node_pad_set, 1)
            nc.gpsimd.memset(ident[:, :], 0.0).then_inc(node_pad_set, 1)
            nc.gpsimd.memset(eps[:, :], EPS).then_inc(consts, 1)
            nc.gpsimd.memset(zero[:, :], 0.0).then_inc(consts, 1)
            nc.gpsimd.memset(one[:, :], 1.0).then_inc(consts, 1)
            nc.gpsimd.iota(iota0[:, :], [[1, P]], base=0, channel_multiplier=0,
                           allow_small_or_imprecise_dtypes=True).then_inc(consts, 1)
            nc.gpsimd.iota(part[:, :], [[0, 1]], base=0, channel_multiplier=1,
                           allow_small_or_imprecise_dtypes=True).then_inc(consts, 1)
            nc.gpsimd.iota(block_first[:, :], [[P, NB]], base=0, channel_multiplier=0,
                           allow_small_or_imprecise_dtypes=True).then_inc(consts, 1)
            pool.wait_ge(node_pad_set, 2)
            nc.gpsimd.affine_select(out=ident[:, :], in_=ident[:, :], compare_op=ALU.not_equal, fill=1.0,
                                    base=0, pattern=[[-1, P]], channel_multiplier=1).then_inc(consts, 1)
            last_first = (NCH - 1) * CH
            with pool.Fori(1, NCH // 2) as i:
                for u in range(2):
                    pool.wait_ge(x_in[u], 16 * i)
                    pool.dma_start(nodes[:, bass.ds((2 * i + u) * CH, CH), :], x_chunks[2 * i + u]).then_inc(x_in[u], 16)
            pool.dma_start(nodes[:, last_first:NB - 1, :],
                           x[last_first * P:(NB - 1) * P, :].rearrange("(v p) d -> p v d", p=P)).then_inc(x_last_in, 16)
            pool.dma_start(nodes[0:LAST, NB - 1, :], x[(NB - 1) * P:N, :]).then_inc(x_last_in, 16)
            nc.gpsimd.memset(sums[:, :, :], 0.0).then_inc(sums_clear, 1)
            pool.wait_ge(stored[0], 16 * (NCH // 2 + 1))
            pool.wait_ge(stored[1], 16 * (NCH // 2))
            last_row = pool.to_reg(NB * P - 1)

            def gather_round(i, half):
                pool.wait_ge(rows_ready, i + 1)
                for u in range(SLOTS):
                    if not isinstance(i, int):
                        pool.wait_ge(pair_summed[u], i)
                    pool.sem_inc(pool_carrier, 1)
                    for j in range(J):
                        pool.indirect_dma_start(messages[:, u, j * D:(j + 1) * D], None, table,
                                                bass.IndirectOffsetOnAxis(ap=row_slots[:, half, u * J + j:u * J + j + 1], axis=0),
                                                bounds_check=last_row).then_inc(gathered[u], 16)

            gather_round(0, 0)

            pool.wait_ge(tables_ready, 1)
            flag = pool.value_load(flag_i[0:1, 0:1], min_val=0, max_val=1)

            def general_load(g, whole):
                for to, a in ((edge_src, src), (edge_type_i, edge_type), (edge_dst, dst)):
                    for first, n, parts in (((0, J, P),) if whole else ((0, (E - g * GE) // P, P),
                                                                       ((E - g * GE) // P, 1, (E - g * GE) % P))):
                        if n == 0 or parts == 0:
                            continue
                        piece = a[0:NG_FULL * GE].rearrange("(g j p) -> g p j", p=P, j=J)[g] if whole else \
                            a[g * GE + first * P:g * GE + first * P + n * parts].rearrange("(j p) -> p j", p=parts)
                        pool.dma_start(to[0:parts, first:first + n], piece,
                                       allow_slow_non_contiguous=True).then_inc(general_in, 16)

            def general_gather():
                for j in range(J):
                    pool.indirect_dma_start(general_rows_sb[:, j * D:(j + 1) * D], None, table,
                                            bass.IndirectOffsetOnAxis(ap=edge_src[:, j:j + 1], axis=0),
                                            bounds_check=last_row).then_inc(general_rows, 16)

            with pool.If(flag > 0):
                pool.sem_inc(general_added, 1)
                with pool.Fori(0, NG_FULL) as g:
                    pool.wait_ge(general_added, g * NB + 1)
                    pool.sem_inc(pool_carrier, 1)
                    general_load(g, True)
                    pool.wait_ge(general_in, 48 * (g + 1))
                    pool.sem_inc(pool_carrier, 1)
                    general_gather()
                pool.wait_ge(general_added, NG_FULL * NB + 1)
                nc.gpsimd.memset(edge_src[:, :], 0).then_inc(general_pads, 1)
                nc.gpsimd.memset(edge_type_i[:, :], 0).then_inc(general_pads, 1)
                nc.gpsimd.memset(edge_dst[:, :], -1).then_inc(general_pads, 1)
                pool.wait_ge(general_pads, 3)
                general_load(NG_FULL, False)
                pool.wait_ge(general_in, 48 * NG_FULL + 96)
                general_gather()
                pool.wait_ge(general_added, (NG_FULL + 1) * NB + 1)

            with pool.Fori(0, ROUNDS // 2) as k:
                gather_round(2 * k + 1, 1)
                gather_round(2 * k + 2, 0)

        @block.scalar
        def _(act):
            for s in (ffn_norm_t, ffn_gelu, slot_cleared):
                act.sem_inc(s, 1)

            def deviate_chunk(c, u):
                act.wait_ge(norm_step, 2 * CH * (c + 1))
                nc.scalar.activation(chunk_deviation[:, u, :], chunk_moments[:, u, :, 1], ACT.Sqrt, bias=eps[:, 0:1]).then_inc(norm_deviation, 1)

            def prepare_chunk(c, u, half):
                act.wait_ge(norm_scaled, 2 * c + 2)
                if not isinstance(c, int) or c > 1:
                    act.wait_ge(stored[u], 16 * half)
                act.sem_inc(wait_carrier, 1)

            def norm_block(c, u, v):
                ins = nc.scalar.activation(stage[:, u * CH + v, :], nodes[:, c * CH + v, :], ACT.Identity,
                                           bias=chunk_shift[:, u, v:v + 1], scale=chunk_rstd[:, u, v:v + 1])
                if v == CH - 1:
                    ins.then_inc(norm_ready, 1)

            def norm_chunk(c, u, half):
                deviate_chunk(c, u)
                prepare_chunk(c, u, half)
                for v in range(CH):
                    norm_block(c, u, v)

            def take_tables():
                for n in range(2 * GT):
                    k, t = n // GT, n % GT
                    to = (gather_rows, keys)[k]
                    width = min(P, NGT - t * P)
                    act.wait_ge(slab_turned, n + 1)
                    nc.scalar.activation(to[:, t * P:t * P + width, :].rearrange("p g j -> p j g"),
                                         banks[n % 2][:, :].rearrange("p (j g) -> p j g", j=J)[:, :, 0:width],
                                         ACT.Copy).then_inc(slab_taken, 1)

            act.wait_ge(consts, CONSTS)
            norm_chunk(0, 0, 0)
            norm_chunk(1, 1, 0)
            act.wait_ge(edges_in, 16 * 9)
            nc.scalar.activation(src_f, src_s, ACT.Copy).then_inc(src_f_ready, 1)
            take_tables()
            act.wait_ge(slab_taken, 2 * GT)
            for i in range(2):
                nc.scalar.activation(row_slots[:, i, :], gather_rows[:, i * SLOTS:(i + 1) * SLOTS, :].rearrange("p g j -> p (g j)"),
                                     ACT.Copy).then_inc(rows_ready, 1)
            with act.Fori(1, NCH // 2) as i:
                norm_chunk(2 * i, 0, i)
                norm_chunk(2 * i + 1, 1, i)
            norm_chunk(NCH - 1, 0, NCH // 2)

            def close(b):
                slot = (b & 1) * OPEN
                act.wait_ge(carried, b + 1)
                act.wait_ge(agg_ready, b + 1)
                act.sem_inc(wait_carrier, 1)
                nc.scalar.activation(closed[:, :, :], sums[:, :, bass.ds(slot, P)], ACT.Copy).then_inc(closed_ready, 1)
                act.wait_ge(loop_turned, b + 1)
                nc.scalar.activation(normed_x_t[:, :, :].rearrange("p k n -> p (k n)"), banks[4][:, 0:D],
                                     ACT.Copy).then_inc(loop_t_ready, 1)
                act.wait_ge(closed_ready, b + 1)
                act.sem_inc(wait_carrier, 1)
                nc.scalar.activation(sums[:, :, bass.ds(slot, OPEN)], zero[:, 0:1].unsqueeze(1).broadcast_to([P, KR, OPEN]),
                                     ACT.Copy).then_inc(slot_cleared, 1)

            def ffn_deviate_and_turn(b):
                act.wait_ge(ffn_step, FFN_STEPS * b + 3)
                nc.scalar.activation(deviation[:, :], moments[:, 1:2], ACT.Sqrt, bias=eps[:, 0:1]).then_inc(ffn_deviation, 1)
                act.wait_ge(ffn_turned, b + 2)
                act.wait_ge(ffn_up, b + 1)
                nc.scalar.activation(normed_t[:, :, :].rearrange("p k n -> p (k n)"), banks[4][:, 0:D],
                                     ACT.Copy).then_inc(ffn_norm_t, 1)

            def ffn_activate(b):
                act.wait_ge(ffn_up, b + 2)
                act.wait_ge(ffn_down, b + 1)
                for m in range(HC):
                    last = nc.scalar.activation(hidden[:, m, :], banks[5 + m // 4][:, m % 4 * P:(m % 4 + 1) * P],
                                                ACT.Gelu_apprx_tanh, bias=b1_col[:, m:m + 1])
                last.then_inc(ffn_gelu, 1)

            act.wait_ge(small_in, 16 * 5)
            act.wait_ge(tables_ready, 1)

            def refill_rows(i):
                for u in range(SLOTS):
                    act.wait_ge(gathered[u], 64 * i)
                act.sem_inc(wait_carrier, 1)
                nc.scalar.activation(row_slots[:, bass.ds((i + 1) & 1, 1), :].rearrange("p h n -> p (h n)"),
                                     gather_rows[:, bass.ds(SLOTS * i + SLOTS, SLOTS), :].rearrange("p g j -> p (g j)"),
                                     ACT.Copy).then_inc(rows_ready, 1)

            def finish_round(i):
                (enters, follows, _), blocks, _ = phases(act, i)
                with act.If(enters > 0):
                    close(blocks[0])
                with act.If(follows > 0):
                    ffn_deviate_and_turn(blocks[1])
                    ffn_activate(blocks[1])

            with act.Fori(1, ROUNDS) as i:
                refill_rows(i)
                finish_round(i)
            for n in range(DRAIN):
                finish_round(ROUNDS + n)
            many_left = act.value_load(many_left_i[0:1, 0:1], min_val=0, max_val=1)
            with act.If(many_left > 0):
                with act.Fori(ROUNDS + DRAIN, STEPS) as i:
                    finish_round(i)

        @block.tensor
        def _(pe):
            for s in (ffn_turned, ffn_up, ffn_down, agg_ready):
                pe.sem_inc(s, 1)
            pe.wait_ge(consts, CONSTS)

            def turn_tables(k):
                slab = (src_f, key_s)[k]
                pe.wait_ge((src_f_ready, keys_flat)[k], 1)
                for t in range(GT):
                    n = k * GT + t
                    if n > 1:
                        pe.wait_ge(slab_taken, n - 1)
                    for j in range(J):
                        last = nc.tensor.transpose(banks[n % 2][:, j * P:(j + 1) * P], slab[:, t, j * P:(j + 1) * P], ident[:, :])
                    last.then_inc(slab_turned, 1)

            turn_tables(0)
            pe.wait_ge(keys_flat, 1)
            for h, bank in ((0, 4), (1, 7)):
                for t in range(GT):
                    last = nc.tensor.matmul(banks[bank][0:1, t * P:(t + 1) * P], gmin[:, t, h:h + 1],
                                            ident[:, :], start=True, stop=True)
            last.then_inc(spread, 1)
            turn_tables(1)
            pe.wait_ge(bad_ready, 1)
            pe.wait_ge(slab_taken, 2 * GT)
            nc.tensor.matmul(banks[0][:, 0:1], one_rows, bad[:, :], start=True, stop=True).then_inc(bad_total, 1)

            pe.wait_ge(tables_ready, 1)

            def general_pair(g):
                for j in range(J):
                    n = J * g + j
                    pe.wait_ge(general_rows, 64 * (g + 1))
                    pe.wait_ge(general_message, n + 1)
                    for k in range(KC):
                        last = nc.tensor.transpose(banks[5][:, k * P:(k + 1) * P],
                                                   general_rows_sb[:, j * D + k * P:j * D + (k + 1) * P], ident[:, :])
                    last.then_inc(general_turned, 1)
                    pe.wait_ge(general_t, n + 1)
                    for q in range(4):
                        for k in range(KC):
                            last = nc.tensor.matmul(banks[q][:, :], normed_t[:, k, :], rel_sb[:, k, q * BANK:(q + 1) * BANK],
                                                    start=(k == 0), stop=(k == KC - 1))
                    last.then_inc(general_products, 1)
                pe.wait_ge(general_message, J * g + J + 1)
                pe.sem_inc(wait_carrier, 1)
                with pe.Fori(0, NB) as b:
                    n = g * NB + b
                    pe.wait_ge(general_onehot, n + 1)
                    for j in range(J):
                        last = nc.tensor.matmul(banks[4][:, 0:D], onehot[:, SLOTS - 1, j, :], general_messages[:, j * D:(j + 1) * D],
                                                start=(j == 0), stop=(j == J - 1))
                    last.then_inc(general_summed, 1)

            flag = pe.value_load(flag_i[0:1, 0:1], min_val=0, max_val=1)
            with pe.If(flag > 0):
                pe.wait_ge(rel_in, 16 * KC)
                with pe.Fori(0, NG_FULL + 1) as g:
                    general_pair(g)

            def sum_pair(i, u):
                pe.wait_ge(onehot_ready[u // 2], i + 1)
                pe.wait_ge(gathered[u], 64 * (i + 1))
                if not isinstance(i, int):
                    pe.wait_ge(sum_taken[u], 2 * i)
                for h in range(GP):
                    for k in range(KC):
                        for e in range(J // GP):
                            j = h * (J // GP) + e
                            last = nc.tensor.matmul(banks[u][:, h * D + k * P:h * D + (k + 1) * P],
                                                    messages[:, u, j * D + k * P:j * D + (k + 1) * P], onehot[:, u, j, :],
                                                    start=(e == 0), stop=(e == J // GP - 1))
                last.then_inc(pair_summed[u], 1)

            def loop_turn(b):
                pe.wait_ge(normed_x_in, 16 * b + 16)
                pe.wait_ge(agg_taken, b + 1)
                for k in range(KC):
                    last = nc.tensor.transpose(banks[4][:, k * P:(k + 1) * P], normed_x[:, k * P:(k + 1) * P], ident[:, :])
                last.then_inc(loop_turned, 1)

            def relation_products(b):
                pe.wait_ge(closed_ready, b + 1)
                pe.wait_ge(loop_t_ready, b + 1)
                pe.wait_ge(ffn_norm_t, b + 1)
                for n in range(KR):
                    k, r = n // R, n % R
                    last = nc.tensor.matmul(banks[4][:, 0:D], closed[:, n, :], rel_sb[:, k, r * D:(r + 1) * D],
                                            start=(n == 0), stop=False)
                for k in range(KC):
                    last = nc.tensor.matmul(banks[4][:, 0:D], normed_x_t[:, k, :], loop_sb[:, k, :],
                                            start=False, stop=(k == KC - 1))
                last.then_inc(agg_ready, 1)

            def ffn_turn(b):
                pe.wait_ge(ffn_norm, b + 1)
                pe.wait_ge(ffn_norm_t, b + 1)
                for k in range(KC):
                    last = nc.tensor.transpose(banks[4][:, k * P:(k + 1) * P], normed[:, k * P:(k + 1) * P], ident[:, :])
                last.then_inc(ffn_turned, 1)

            def ffn_first(b):
                pe.wait_ge(ffn_norm_t, b + 2)
                pe.wait_ge(ffn_gelu, b + 1)
                for m in range(HC):
                    for k in range(KC):
                        last = nc.tensor.matmul(banks[5 + m // 4][:, m % 4 * P:(m % 4 + 1) * P],
                                                w1_sb[:, k, m * P:(m + 1) * P], normed_t[:, k, :],
                                                start=(k == 0), stop=(k == KC - 1))
                last.then_inc(ffn_up, 1)

            def ffn_second(b):
                pe.wait_ge(ffn_gelu, b + 2)
                pe.wait_ge(ffn_done, 2 * b + 1)
                for m in range(HC):
                    last = nc.tensor.matmul(banks[7][:, 0:D], hidden[:, m, :], w2_sb[:, m, :],
                                            start=(m == 0), stop=(m == HC - 1))
                last.then_inc(ffn_down, 1)

            def tensor_round(i, sum_one):
                (enters, follows, leaves), blocks, _ = phases(pe, i)
                sum_one(0)
                with pe.If(leaves > 0):
                    ffn_second(blocks[2])
                sum_one(1)
                with pe.If(enters > 0):
                    loop_turn(blocks[0])
                sum_one(2)
                with pe.If(follows > 0):
                    ffn_turn(blocks[1])
                sum_one(3)
                with pe.If(follows > 0):
                    ffn_first(blocks[1])
                with pe.If(enters > 0):
                    relation_products(blocks[0])

            for u in range(SLOTS):
                sum_pair(0, u)
            pe.wait_ge(rel_in, 16 * KC)
            pe.wait_ge(ffn_w_in, 32)
            pe.wait_ge(loop_in, 16)
            with pe.Fori(1, ROUNDS) as i:
                tensor_round(i, lambda u: sum_pair(i, u))
            for n in range(DRAIN):
                tensor_round(ROUNDS + n, lambda u: None)
            many_left = pe.value_load(many_left_i[0:1, 0:1], min_val=0, max_val=1)
            with pe.If(many_left > 0):
                with pe.Fori(ROUNDS + DRAIN, STEPS) as i:
                    tensor_round(i, lambda u: None)

            for r in range(8):
                pe.wait_ge(counts_in, r + 1)
                nc.tensor.matmul(banks[0][:, 0:15], one_rows, pick_counts[:, :], start=True, stop=True).then_inc(counts_out, 1)
            pe.wait_ge(counts_in, 9)
            nc.tensor.matmul(banks[0][:, 0:1], one_rows, above_count[:, :], start=True, stop=True)
            nc.tensor.matmul(banks[1][:, 0:NB], one_rows, tied[:, :], start=True, stop=True)
            nc.tensor.matmul(banks[2][:, 0:NB], before[:, :], tied[:, :], start=True, stop=True).then_inc(counts_out, 1)

        @block.vector
        def _(dve):
            V = nc.vector
            count = {}
            for s in (agg_taken, ffn_done):
                dve.sem_inc(s, 1)

            def link(s, ins):
                count[s.name] = count.get(s.name, 0) + 1
                ins.then_inc(s, 1)
                dve.wait_ge(s, count[s.name])

            def moments_of(c, u):
                if not isinstance(c, int) or c > 1:
                    dve.wait_ge(norm_ready, c - 1)
                if not isinstance(c, int) or c > 0:
                    dve.wait_ge(norm_step, 2 * CH * c)
                    dve.sem_inc(wait_carrier, 1)
                for v in range(CH):
                    V.bn_stats(chunk_stats[:, v, :], nodes[:, c * CH + v, :]).then_inc(norm_step, 1)
                dve.wait_ge(norm_step, 2 * CH * c + CH)
                dve.sem_inc(wait_carrier, 1)
                for v in range(CH):
                    V.bn_aggr(chunk_moments[:, u, v, :], chunk_stats[:, v, :]).then_inc(norm_step, 1)

            def factors_of(c, u):
                dve.wait_ge(norm_deviation, c + 1)
                V.reciprocal(chunk_rstd[:, u, :], chunk_deviation[:, u, :]).then_inc(norm_scaled, 1)
                dve.wait_ge(norm_scaled, 2 * c + 1)
                V.scalar_tensor_tensor(chunk_shift[:, u, :], chunk_moments[:, u, :, 0], -1.0, chunk_rstd[:, u, :], ALU.mult, ALU.mult).then_inc(norm_scaled, 1)

            def index(ins):
                link(index_step, ins)

            def row(ins):
                link(row_step, ins)

            def index_stage():
                dve.wait_ge(edges_in, 16 * 9)
                last_tile = key_s[:, GT - 1, :]
                index(V.tensor_scalar(last_tile, dst_s[:, GT - 1, :], 0.0, 16384.0, ALU.is_lt, ALU.mult))
                index(V.tensor_tensor(last_tile, last_tile, dst_s[:, GT - 1, :], ALU.add))
                dst_g, key_g, type_g = [a.rearrange("p t (h e) -> p (t h) e", h=GP) for a in (dst_s, key_s, type_s)]
                first, span = (a[:, :, :].rearrange("p t h -> p (t h)") for a in (gmin, gspan))
                whole = GP * (GT - 1)
                index(V.tensor_reduce(first[:, 0:whole], dst_g[:, 0:whole, :], AX.X, ALU.min))
                index(V.tensor_reduce(first[:, whole:], key_g[:, whole:, :], AX.X, ALU.min))
                index(V.tensor_reduce(span, dst_g, AX.X, ALU.max))
                index(V.tensor_scalar_min(first, first, float(N - 1)))
                index(V.tensor_tensor(span, span, first, ALU.subtract))
                index(V.tensor_tensor(key_g, dst_g, first.unsqueeze(2).broadcast_to([P, GT * GP, GE // GP]), ALU.subtract))
                V.scalar_tensor_tensor(key_g, type_g, float(W), key_g, ALU.mult, ALU.add).then_inc(keys_flat, 1)
                index(V.tensor_scalar(span, span, float(W), None, ALU.is_ge))
                index(V.tensor_reduce(bad[:, :], span, AX.X, ALU.add))

            def window_stage():
                dve.wait_ge(src_f_ready, 1)
                dve.wait_ge(spread, 1)
                V.tensor_copy(gmin_i[:, 0, :], banks[4][0:1, :]).then_inc(row_step, 1)
                V.tensor_copy(gmin_i[:, 1, :], banks[7][0:1, :]).then_inc(row_step, 1)
                count[row_step.name] = 2
                dve.wait_ge(row_step, 2)
                row(V.tensor_scalar(offset_i, gmin_i, P - 1, None, ALU.bitwise_and))
                row(V.tensor_scalar(block_i, gmin_i, P.bit_length() - 1, None, ALU.logical_shift_right))
                row(V.tensor_scalar(parity_i, block_i, 1, None, ALU.bitwise_and))
                row(V.scalar_tensor_tensor(offset_i, parity_i, float(OPEN), offset_i, ALU.mult, ALU.add))
                row(V.scalar_tensor_tensor(position[:, :], offset_i[:, 1, 0:NG], 512.0, offset_i[:, 0, 0:NG], ALU.mult, ALU.add))
                row(V.tensor_copy(block_f, block_i))

            def order_stage():
                row(V.memset(goal, float(NB)))
                row(V.tensor_copy(goal[:, 0:ROUNDS], block_f[:, 0, 0:NG].rearrange("p (i u) -> p i u", u=SLOTS)[:, :, 1]))
                row(V.memset(goal[:, 0:1], 0.0))
                row(V.memset(steps_one, 1.0))
                row(V.memset(steps_goal, 0.0))
                row(V.tensor_tensor_scan(highest_goal, goal, steps_goal, 0.0, ALU.max, ALU.max))
                row(V.memset(entered[:, 0:3], 0.0))
                row(V.tensor_tensor_scan(entered[:, 3:3 + STEPS], steps_one, highest_goal, 0.0, ALU.add, ALU.min))
                e = [entered[:, n:n + STEPS] for n in range(4)]
                row(V.tensor_scalar(steps_goal, e[2], float(FIELD), None, ALU.mult))
                row(V.scalar_tensor_tensor(steps_goal, e[3], float(FIELD), steps_goal, ALU.mult, ALU.add))
                row(V.scalar_tensor_tensor(steps_goal, e[1], float(2 * FIELD), steps_goal, ALU.mult, ALU.add))
                row(V.scalar_tensor_tensor(round_code[:, :], e[0], float(1 - 4 * FIELD), steps_goal, ALU.mult, ALU.add))
                row(V.tensor_scalar(many_left_i[:, :], entered[:, 3 + ROUNDS + DRAIN - 3:3 + ROUNDS + DRAIN - 2], float(NB), None, ALU.is_lt))
                by_round = [a[:, 0, 0:NG].rearrange("p (i u) -> p i u", u=SLOTS) for a in (lowest, highest)]
                past, now = (entered[:, 2 + n:2 + n + ROUNDS].unsqueeze(2) for n in range(2))
                row(V.tensor_copy(by_round[0][:, :, 0:1], past))
                row(V.tensor_copy(by_round[0][:, :, 1:4], now.broadcast_to([1, ROUNDS, 3])))
                row(V.tensor_scalar(by_round[1][:, :, 0:2], past.broadcast_to([1, ROUNDS, 2]), 1.0, None, ALU.add))
                row(V.tensor_scalar(by_round[1][:, :, 2:4], now.broadcast_to([1, ROUNDS, 2]), 1.0, None, ALU.add))
                for h in range(GP):
                    of_groups = block_f[:, h, 0:NG]
                    row(V.tensor_tensor(lowest[:, 1, 0:NG], lowest[:, 0, 0:NG], of_groups, ALU.is_gt))
                    row(V.tensor_tensor(highest[:, 1, 0:NG], of_groups, highest[:, 0, 0:NG], ALU.is_gt))
                    row(V.tensor_tensor(lowest[:, 1, 0:NG], lowest[:, 1, 0:NG], highest[:, 1, 0:NG], ALU.add))
                    row(V.tensor_reduce(violations[:, :], lowest[:, 1, 0:NG], AX.X, ALU.add))
                    row(V.tensor_tensor(bad[0:1, :], bad[0:1, :], violations[:, :], ALU.add))
                dve.sem_inc(bad_ready, 1)

            def norm_chunk(c, u, loads):
                dve.wait_ge(x_in[u], 16 * loads)
                moments_of(c, u)
                factors_of(c, u)

            norm_chunk(0, 0, 1)
            norm_chunk(1, 1, 1)
            index_stage()
            with dve.Fori(1, NCH // 2) as i:
                norm_chunk(2 * i, 0, i + 1)
                norm_chunk(2 * i + 1, 1, i + 1)
            dve.wait_ge(x_last_in, 32)
            moments_of(NCH - 1, 0)
            factors_of(NCH - 1, 0)
            window_stage()
            order_stage()
            dve.wait_ge(bad_total, 1)
            row(V.tensor_scalar(regular[:, :], banks[0][:, 0:1], 0.0, None, ALU.is_equal))
            row(V.tensor_scalar(flag_i[:, :], regular[0:1, :], -1.0, 1.0, ALU.mult, ALU.add))
            dve.sem_inc(tables_ready, 1)

            def build(i, half):
                at = slice(SLOTS * i + 2 * half, SLOTS * i + 2 * half + 2) if isinstance(i, int) else \
                    bass.ds(SLOTS * i + 2 * half, 2)
                V.tensor_tensor(onehot[:, 2 * half:2 * half + 2, :, :].rearrange("p u j c -> p (u j) c"),
                                iota0[:, :].unsqueeze(1).broadcast_to([P, 2 * J, P]),
                                keys[:, at, :].rearrange("p g j -> p (g j)").unsqueeze(2).broadcast_to([P, 2 * J, P]),
                                ALU.is_equal).then_inc(onehot_ready[half], 1)

            dve.wait_ge(slab_taken, 2 * GT)
            build(0, 0)
            dve.wait_ge(sums_clear, 1)

            flag = dve.value_load(flag_i[0:1, 0:1], min_val=0, max_val=1)
            with dve.If(flag > 0):
                for s in (general_message, general_cast):
                    dve.sem_inc(s, 1)

                def general_pair(g):
                    dve.wait_ge(general_rows, 64 * (g + 1))
                    V.tensor_copy(edge_type_f[:, :], edge_type_i[:, :]).then_inc(general_cast, 1)
                    V.tensor_copy(edge_dst_f[:, :], edge_dst[:, :]).then_inc(general_cast, 1)
                    dve.wait_ge(general_cast, (2 + J * R) * g + 3)
                    for j in range(J):
                        n = J * g + j
                        V.tensor_scalar(of_relation[:, :], iota0[:, 0:R], edge_type_f[:, j:j + 1], None, ALU.is_equal).then_inc(general_cast, 1)
                        dve.wait_ge(general_turned, n + 1)
                        V.tensor_copy(normed_t[:, :, :].rearrange("p k n -> p (k n)"), banks[5][:, 0:D]).then_inc(general_t, 1)
                        dve.wait_ge(general_products, n + 1)
                        for r in range(R):
                            done = (2 + J * R) * g + 3 + j * R + r + 1
                            dve.wait_ge(general_cast, done)
                            to = general_messages[:, j * D:(j + 1) * D]
                            product = banks[r // 2][:, r % 2 * D:(r % 2 + 1) * D]
                            if r == 0:
                                ins = V.tensor_scalar(to, product, of_relation[:, 0:1], None, ALU.mult)
                            else:
                                ins = V.scalar_tensor_tensor(to, product, of_relation[:, r:r + 1], to, ALU.mult, ALU.add)
                            ins.then_inc(general_message if r == R - 1 else general_cast, 1)
                        dve.wait_ge(general_message, n + 2)
                        dve.sem_inc(wait_carrier, 1)
                    with dve.Fori(0, NB) as b:
                        n = g * NB + b
                        dve.wait_ge(general_added, n + 1)
                        V.tensor_scalar(shifted[:, :], edge_dst_f[:, :], block_first[:, bass.ds(b, 1)], None,
                                        ALU.subtract).then_inc(general_shift, 1)
                        dve.wait_ge(general_shift, n + 1)
                        for j in range(J):
                            last = V.tensor_scalar(onehot[:, SLOTS - 1, j, :], iota0[:, :], shifted[:, j:j + 1], None, ALU.is_equal)
                        last.then_inc(general_onehot, 1)
                        dve.wait_ge(general_summed, n + 1)
                        V.scalar_tensor_tensor(nodes[:, b, :], banks[4][:, 0:D], SCALE, nodes[:, b, :],
                                               ALU.mult, ALU.add).then_inc(general_added, 1)

                with dve.Fori(0, NG_FULL + 1) as g:
                    general_pair(g)
                dve.wait_ge(general_added, (NG_FULL + 1) * NB + 1)

            def add_pair(i, u):
                if u == 0:
                    build(i, 1)
                elif u == 2:
                    for v in range(2):
                        dve.wait_ge(pair_summed[v], i + 1)
                    dve.sem_inc(wait_carrier, 1)
                    build(i + 1, 0)
                g = SLOTS * i + u
                at = slice(g, g + 1) if isinstance(g, int) else bass.ds(g, 1)
                packed = dve.value_load(position[0:1, at], min_val=0, max_val=512 * 512 - 1)
                to = [(packed & 511).with_bounds(min_val=0, max_val=OPEN + P - 1), (packed >> 9).with_bounds(min_val=0, max_val=OPEN + P - 1)]
                dve.wait_ge(pair_summed[u], i + 1)
                if u:
                    dve.wait_ge(sum_taken[u - 1], 2 * (i + 1))
                elif not isinstance(i, int):
                    dve.wait_ge(sum_taken[SLOTS - 1], 2 * i)
                for h in range(GP):
                    if h:
                        dve.wait_ge(sum_taken[u], 2 * i + 1)
                    V.scalar_tensor_tensor(sums[:, :, bass.ds(to[h], W)],
                                           banks[u][:, h * D:(h + 1) * D].rearrange("p (n m) -> p n m", m=W),
                                           regular[:, 0:1], sums[:, :, bass.ds(to[h], W)],
                                           ALU.mult, ALU.add).then_inc(sum_taken[u], 1)

            def carry(b, all_added):
                slot = (b & 1) * OPEN
                for s, n in all_added:
                    dve.wait_ge(s, n)
                dve.wait_ge(slot_cleared, b + 1)
                V.tensor_tensor(sums[:, :, bass.ds(OPEN - slot, W)], sums[:, :, bass.ds(slot + P, W)],
                                sums[:, :, bass.ds(OPEN - slot, W)], ALU.add).then_inc(carried, 1)
                dve.wait_ge(carried, b + 1)
                dve.sem_inc(wait_carrier, 1)

            def step(b, n, ins):
                ins.then_inc(ffn_step, 1)
                dve.wait_ge(ffn_step, FFN_STEPS * b + n)

            def ffn_enter(b):
                dve.wait_ge(agg_ready, b + 2)
                V.scalar_tensor_tensor(x1[:, :], banks[4][:, 0:D], SCALE, nodes[:, b, :], ALU.mult, ALU.add).then_inc(agg_taken, 1)
                dve.wait_ge(agg_taken, b + 2)
                step(b, 1, V.tensor_tensor(x1[:, :], x1[:, :], bias_b[:, :], ALU.add))
                V.bn_stats(stats[:, :], x1[:, :]).then_inc(ffn_step, 1)
                dve.wait_ge(ffn_step, FFN_STEPS * b + 2)
                dve.sem_inc(wait_carrier, 1)
                step(b, 3, V.bn_aggr(moments[:, :], stats[:, :]))
                dve.wait_ge(ffn_deviation, b + 1)
                step(b, 4, V.reciprocal(rstd[:, 0:1], deviation[:, :]))
                dve.wait_ge(ffn_turned, b + 1)
                V.tensor_scalar(normed[:, :], x1[:, :], moments[:, 0:1], rstd[:, 0:1],
                                ALU.subtract, ALU.mult).then_inc(ffn_norm, 1)
                dve.wait_ge(ffn_norm, b + 1)
                V.tensor_tensor(nodes[:, b, :], x1[:, :], normed[:, :], ALU.add).then_inc(ffn_step, 1)
                dve.wait_ge(ffn_step, FFN_STEPS * b + 5)
                V.tensor_tensor_reduce(out=x1[:, :], in0=normed[:, :], in1=wr_b[:, :], scale=1.0, scalar=0.0,
                                       op0=ALU.mult, op1=ALU.add, accum_out=w_block[:, 0:1]).then_inc(ffn_step, 1)
                dve.wait_ge(ffn_step, FFN_STEPS * b + 6)
                V.tensor_scalar(w_all[:, bass.ds(b, 1)], w_block[:, 0:1], br_b[:, 0:1], None, ALU.add).then_inc(ffn_step, 1)

            def ffn_leave(b):
                dve.wait_ge(ffn_step, FFN_STEPS * b + 7)
                dve.wait_ge(ffn_down, b + 2)
                V.tensor_tensor(acc[:, b, :], banks[7][:, 0:D], b2_b[:, :], ALU.add).then_inc(ffn_done, 1)
                dve.wait_ge(ffn_done, 2 * b + 2)
                V.tensor_scalar(acc[:, b, :], acc[:, b, :], w_all[:, bass.ds(b, 1)],
                                None, ALU.mult).then_inc(ffn_done, 1)

            def finish_round(i, add_one, all_added, wait_cleared):
                (enters, follows, leaves), blocks, entered_after = phases(dve, i)
                add_one(0)
                with dve.If(enters > 0):
                    carry(blocks[0], all_added)
                with dve.If(follows > 0):
                    ffn_enter(blocks[1])
                add_one(1)
                with dve.If(leaves > 0):
                    ffn_leave(blocks[2])
                if wait_cleared:
                    dve.wait_ge(slot_cleared, entered_after + 1)
                    dve.sem_inc(wait_carrier, 1)
                add_one(2)
                add_one(3)

            def routing_constants():
                link(pick_step, V.tensor_scalar(before[:, :], iota0[:, :], part[:, 0:1], None, ALU.is_gt))
                link(pick_step, V.memset(zeros[:, :], 0.0))
                link(pick_step, V.tensor_scalar(real[:, :], part[:, :], float(LAST), None, ALU.is_lt))
                link(pick_step, V.tensor_scalar(pad_key[:, :], real[:, :], 40000.0, -40000.0, ALU.mult, ALU.add))
                link(pick_step, V.tensor_scalar(digits[:, :], iota0[:, 0:15], 1.0, None, ALU.add))
                link(pick_step, V.memset(tie_base[:, 0:1], 0.0))
                link(pick_step, V.memset(floor_[:, :], -32768.0))

            dve.wait_ge(small_in, 16 * 5)
            for u in range(SLOTS):
                add_pair(0, u)
            with dve.Fori(1, ROUNDS) as i:
                finish_round(i, lambda u: add_pair(i, u), ((sum_taken[0], 2 * (i + 1)),), True)
            for n in range(DRAIN):
                finish_round(ROUNDS + n, lambda u: None, ((sum_taken[SLOTS - 1], 2 * ROUNDS),), False)
                if n == 0:
                    routing_constants()
            many_left = dve.value_load(many_left_i[0:1, 0:1], min_val=0, max_val=1)
            with dve.If(many_left > 0):
                with dve.Fori(ROUNDS + DRAIN, STEPS) as i:
                    finish_round(i, lambda u: None, ((sum_taken[SLOTS - 1], 2 * ROUNDS),), False)
            dve.wait_ge(ffn_done, 2 * NB + 1)

            w_bits = w_all[:, :].bitcast(I32)
            link(pick_step, V.tensor_scalar(sign_i[:, :], w_bits, 31, 0x7FFFFFFF, ALU.arith_shift_right, ALU.bitwise_and))
            link(pick_step, V.tensor_tensor(key_i[:, :], w_bits, sign_i[:, :], ALU.bitwise_xor))
            link(pick_step, V.tensor_scalar(half_i[:, :], key_i[:, :], 16, None, ALU.arith_shift_right))
            link(pick_step, V.tensor_copy(key_hi[:, :], half_i[:, :]))
            link(pick_step, V.tensor_scalar(half_i[:, :], key_i[:, :], 0xFFFF, None, ALU.bitwise_and))
            link(pick_step, V.tensor_copy(key_lo[:, :], half_i[:, :]))
            link(pick_step, V.tensor_scalar(key_hi[:, NB - 1:NB], key_hi[:, NB - 1:NB], real[:, 0:1], pad_key[:, 0:1], ALU.mult, ALU.add))

            def radix_round(r, keys, shift):
                link(pick_step, V.tensor_scalar(candidates[:, :], digits[:, :], float(1 << shift), floor_[:, 0:1], ALU.mult, ALU.add))
                link(pick_step, V.tensor_tensor(compared[:, :, :], keys.unsqueeze(1).broadcast_to([P, 15, NB]),
                                                candidates[:, :].unsqueeze(2).broadcast_to([P, 15, NB]), ALU.is_ge))
                V.tensor_reduce(pick_counts[:, :], compared[:, :, :], AX.X, ALU.add).then_inc(counts_in, 1)
                dve.wait_ge(counts_out, r + 1)
                link(pick_step, V.tensor_scalar(reached[:, :], banks[0][:, 0:15], float(SELECTED), None, ALU.is_ge))
                link(pick_step, V.tensor_reduce(passed[:, :], reached[:, :], AX.X, ALU.add))
                link(pick_step, V.scalar_tensor_tensor(floor_[:, :], passed[:, :], float(1 << shift), floor_[:, :], ALU.mult, ALU.add))

            for r in range(4):
                radix_round(r, key_hi[:, :], 12 - 4 * r)
            link(pick_step, V.tensor_scalar(above[:, :], key_hi[:, :], floor_[:, 0:1], 65536.0, ALU.is_gt, ALU.mult))
            link(pick_step, V.tensor_scalar(tied[:, :], key_hi[:, :], floor_[:, 0:1], None, ALU.is_equal))
            link(pick_step, V.tensor_scalar(key_lo[:, :], key_lo[:, :], 1.0, None, ALU.add))
            link(pick_step, V.tensor_tensor(key_lo[:, :], key_lo[:, :], tied[:, :], ALU.mult))
            link(pick_step, V.tensor_tensor(key_lo[:, :], key_lo[:, :], above[:, :], ALU.add))
            link(pick_step, V.tensor_scalar(key_lo[:, :], key_lo[:, :], -1.0, None, ALU.add))
            link(pick_step, V.memset(floor_[:, :], 0.0))
            for r in range(4):
                radix_round(4 + r, key_lo[:, :], 12 - 4 * r)
            link(pick_step, V.tensor_scalar(above[:, :], key_lo[:, :], floor_[:, 0:1], None, ALU.is_gt))
            link(pick_step, V.tensor_scalar(tied[:, :], key_lo[:, :], floor_[:, 0:1], None, ALU.is_equal))
            V.tensor_reduce(above_count[:, :], above[:, :], AX.X, ALU.add).then_inc(counts_in, 1)
            dve.wait_ge(counts_out, 9)
            link(pick_step, V.tensor_scalar(quota[:, :], banks[0][:, 0:1], -1.0, float(SELECTED), ALU.mult, ALU.add))
            link(pick_step, V.tensor_copy(key_hi[:, :], banks[1][:, 0:NB]))
            link(pick_step, V.tensor_tensor_scan(tie_base[:, 1:NB + 1], key_hi[:, :], zeros[:, :], 0.0, ALU.add, ALU.add))
            link(pick_step, V.tensor_tensor(keep[:, :], banks[2][:, 0:NB], tie_base[:, 0:NB], ALU.add))
            link(pick_step, V.tensor_scalar(keep[:, :], keep[:, :], quota[:, 0:1], None, ALU.is_lt))
            link(pick_step, V.tensor_tensor(keep[:, :], keep[:, :], tied[:, :], ALU.mult))
            link(pick_step, V.tensor_tensor(keep[:, :], keep[:, :], above[:, :], ALU.add))

            def finish(b):
                at = slice(b, b + 1) if isinstance(b, int) else bass.ds(b, 1)
                V.scalar_tensor_tensor(nodes[:, b, :], acc[:, b, :], keep[:, at], nodes[:, b, :],
                                       ALU.mult, ALU.add).then_inc(output_ready, 1)

            with dve.Fori(0, NB // 4) as q:
                for v in range(4):
                    finish(4 * q + v)
            finish(NB - 1)


_NAMES = ["x", "src", "dst", "edge_type_8", "L0_gnn_weight", "L0_gnn_h_bias", "L0_gnn_loop_weight",
          "L0_ffn_wr", "L0_ffn_br", "L0_ffn_w1", "L0_ffn_b1", "L0_ffn_w2", "L0_ffn_b2"]


def kernel(**inputs):
    import numpy as _np
    import concourse.bacc as _bacc
    from concourse import mybir as _mybir
    from concourse.bass_utils import run_bass_kernel_spmd as _run

    nc = _bacc.Bacc("TRN2", target_bir_lowering=False, num_devices=1)
    arrays, args = {}, []
    for name in _NAMES:
        a = _np.ascontiguousarray(inputs[name])
        arrays[f"in_{name}"] = a
        args.append(nc.dram_tensor(f"in_{name}", a.shape, _mybir.dt.from_np(a.dtype), kind="ExternalInput").ap())
    shape = _np.shape(inputs["x"])
    args.append(nc.dram_tensor("node_out", shape, _mybir.dt.float32, kind="ExternalOutput").ap())
    gnn_ffn_program(nc, *args)
    r = _run(nc, [arrays], core_ids=[0])
    return r.results[0]["node_out"]
```
